# Optimizing a Trainium2 kernel written in Bass

```python
import numpy as np
import jax
import jax.numpy as jnp

def _softmax(x, axis=-1):
    return jax.nn.softmax(x, axis=axis)

def _gelu(x):
    return jax.nn.gelu(x, approximate=True)

def _silu(x):
    return jax.nn.silu(x)

def _sigmoid(x):
    return jax.nn.sigmoid(x)

def _layernorm(x, axis=-1, eps=1e-05):
    m = jnp.mean(x, axis=axis, keepdims=True)
    v = jnp.var(x, axis=axis, keepdims=True)
    return (x - m) / jnp.sqrt(v + eps)

def _scatter_add(tgt, idx, src, axis=0):
    return tgt.at[idx].add(src)

def _segment_sum(src, seg, n):
    return jax.ops.segment_sum(src, seg, n)
kernel_name = 'mk_flamingo_gated_d1_seqx_r4_9c292c'

def setup_inputs(seed: int=0):
    np.random.seed(seed)
    _w = jnp.asarray

    def _rec_inputs():
        import jax
        import jax.numpy as jnp
        _rk = jax.random.key(seed)
        x = 7.22e-05 + 1 * jax.random.normal(jax.random.fold_in(_rk, 1), (16, 128, 256), jnp.float32)
        _lenS = 128 - jax.random.randint(jax.random.fold_in(_rk, 7), (16,), 0, max(1, 128 // 4) + 1, jnp.int32)
        _lenS2 = 128 - jax.random.randint(jax.random.fold_in(_rk, 8), (16,), 0, max(1, 128 // 4) + 1, jnp.int32)
        _ctx_1024P = jax.random.normal(jax.random.fold_in(_rk, 11), (16, 16, 256), jnp.float32)
        _ctx_1024c = jax.random.dirichlet(jax.random.fold_in(_rk, 511), 0.3 * jnp.ones((16,), jnp.float32), (16, 128))
        _ctx_1024t = jnp.einsum('bsk,bkd->bsd', _ctx_1024c, _ctx_1024P)
        _ctx_1024t = _ctx_1024t * jax.lax.rsqrt(jnp.mean(jnp.square(_ctx_1024t)) + 1e-12) * 0.953939
        ctx_1024 = -1.52775e-05 + 0.999936 * (_ctx_1024t + 0.3 * jax.random.normal(jax.random.fold_in(_rk, 611), (16, 128, 256), jnp.float32))
        _validS = jnp.arange(128)[None, :] < _lenS[:, None]
        _validS2 = jnp.arange(128)[None, :] < _lenS2[:, None]
        _causal = jnp.tril(jnp.ones((128, 128), dtype=bool))
        mask_BxS2_bk0 = jnp.logical_not(jnp.broadcast_to(_validS2[:, :], (16, 128)))
        _g = jax.random.normal(jax.random.fold_in(_rk, 9001), (2, 1), jnp.float32)
        _g = jnp.sign(_g) * jnp.maximum(jnp.abs(_g), 1.0) + (_g == 0) * 1.0
        g_xattn = _g[0]
        g_ffn = _g[1]
        return (x, ctx_1024, mask_BxS2_bk0, g_xattn, g_ffn)
    x, ctx_1024, mask_BxS2_bk0, g_xattn, g_ffn = _rec_inputs()

    def _L0_xattn_setup():
        import jax, jax.numpy as jnp
        import numpy as np
        D_MODEL = 256
        N_HEADS = 1
        HEAD_DIM = D_MODEL // N_HEADS
        N, LEN_Q, LEN_IN = (8, 256, 1024)
        key = jax.random.key(seed)
        ks = jax.random.split(key, 7)
        s = 1.0 / np.sqrt(D_MODEL)
        return {'query': jax.random.normal(ks[0], (N, LEN_Q, D_MODEL), dtype=jnp.float32), 'input_flatten': jax.random.normal(ks[1], (N, LEN_IN, D_MODEL), dtype=jnp.float32), 'input_padding_mask': jax.random.randint(ks[2], (N, LEN_IN), 0, 2).astype(bool), 'Wq': jax.random.normal(ks[3], (D_MODEL, D_MODEL), dtype=jnp.float32) * s, 'bq': jnp.zeros((D_MODEL,), dtype=jnp.float32), 'Wk': jax.random.normal(ks[4], (D_MODEL, D_MODEL), dtype=jnp.float32) * s, 'bk': jnp.zeros((D_MODEL,), dtype=jnp.float32), 'Wo': jax.random.normal(ks[5], (D_MODEL, D_MODEL), dtype=jnp.float32) * s, 'bo': jnp.zeros((D_MODEL,), dtype=jnp.float32)}
    _L0_xattn_all = _L0_xattn_setup()
    _L0_xattn_in = {k: v for k, v in _L0_xattn_all.items() if k in ('Wq', 'bq', 'Wk', 'bk', 'Wo', 'bo')}
    del _L0_xattn_all

    def _L0_ffn_setup():
        import jax, jax.numpy as jnp
        import numpy as np
        MAX_VAL = 100.0
        key = jax.random.key(seed)
        k1, k2, k3 = jax.random.split(key, 3)
        B, S, D_IN, D_OUT = (4, 2048, 256, 256)
        x = jax.random.normal(k1, (B, S, D_IN), dtype=jnp.float32)
        weights = jax.random.normal(k2, (D_OUT, D_IN), dtype=jnp.float32)
        scale = jnp.ones((D_OUT,), dtype=jnp.float32)
        bias = jax.random.normal(k3, (D_OUT,), dtype=jnp.float32)
        return {'x': x, 'weights': weights, 'scale': scale, 'bias': bias}
    _L0_ffn_all = _L0_ffn_setup()
    _L0_ffn_in = {k: v for k, v in _L0_ffn_all.items() if k in ('weights', 'scale', 'bias')}
    del _L0_ffn_all
    return {'x': x, 'ctx_1024': ctx_1024, 'mask_BxS2_bk0': mask_BxS2_bk0, 'g_xattn': g_xattn, 'g_ffn': g_ffn, 'L0_xattn_Wq': _L0_xattn_in['Wq'], 'L0_xattn_bq': _L0_xattn_in['bq'], 'L0_xattn_Wk': _L0_xattn_in['Wk'], 'L0_xattn_bk': _L0_xattn_in['bk'], 'L0_xattn_Wo': _L0_xattn_in['Wo'], 'L0_xattn_bo': _L0_xattn_in['bo'], 'L0_ffn_weights': _L0_ffn_in['weights'], 'L0_ffn_scale': _L0_ffn_in['scale'], 'L0_ffn_bias': _L0_ffn_in['bias']}

def reference(x, ctx_1024, mask_BxS2_bk0, g_xattn, g_ffn, L0_xattn_Wq, L0_xattn_bq, L0_xattn_Wk, L0_xattn_bk, L0_xattn_Wo, L0_xattn_bo, L0_ffn_weights, L0_ffn_scale, L0_ffn_bias):
    import jax
    import jax.numpy as jnp

    def _L0_xattn_ref(query, input_flatten, input_padding_mask, Wq, bq, Wk, bk, Wo, bo):
        import jax, jax.numpy as jnp
        import numpy as np
        D_MODEL = 256
        N_HEADS = 1
        HEAD_DIM = D_MODEL // N_HEADS
        N, LEN_Q, LEN_IN = (8, 256, 1024)
        n, len_q, _ = query.shape
        len_in = input_flatten.shape[1]
        Q = (query @ Wq.T + bq).reshape(n, len_q, N_HEADS, HEAD_DIM).transpose(0, 2, 1, 3)
        K = (input_flatten @ Wk.T + bk).reshape(n, len_in, N_HEADS, HEAD_DIM).transpose(0, 2, 1, 3)
        scores = jnp.einsum('nhqd,nhkd->nhqk', Q, K)
        scores = jnp.where(input_padding_mask[:, None, None, :], -jnp.inf, scores)
        attn = jax.nn.softmax(scores, axis=-1)
        V = jnp.broadcast_to(input_flatten[:, None], (n, N_HEADS, len_in, D_MODEL))
        out = jnp.einsum('nhql,nhld->nhqd', attn, V)
        out = out.transpose(0, 2, 1, 3).reshape(n, len_q, D_MODEL)
        return out @ Wo.T + bo

    def _L0_ffn_ref(x, weights, scale, bias):
        import jax, jax.numpy as jnp
        import numpy as np
        MAX_VAL = 100.0
        w = (weights >= 0.0).astype(x.dtype) * 2.0 - 1.0
        y = jnp.einsum('bsi,oi->bso', x, w)
        y = y * scale + bias
        y = jnp.clip(y, -MAX_VAL, MAX_VAL)
        return y
    x = x + jnp.tanh(g_xattn[0]) * _L0_xattn_ref(_layernorm(x, axis=-1), ctx_1024, mask_BxS2_bk0, L0_xattn_Wq, L0_xattn_bq, L0_xattn_Wk, L0_xattn_bk, L0_xattn_Wo, L0_xattn_bo)
    x = x + jnp.tanh(g_ffn[0]) * _L0_ffn_ref(_layernorm(x, axis=-1), L0_ffn_weights, L0_ffn_scale, L0_ffn_bias)
    return x

_drawn_inputs = setup_inputs


def setup_inputs(seed=0):
    import zlib

    import numpy as np

    out = dict(_drawn_inputs(seed))
    spreads = {'L0_xattn_bq': (0.0, 0.1),
     'L0_xattn_bk': (0.0, 0.1),
     'L0_xattn_bo': (0.0, 0.1),
     'L0_ffn_scale': (1.0, 0.2)}
    factors = {}
    for name, (base, spread) in spreads.items():
        noise = np.random.default_rng([zlib.crc32(name.encode()), seed]).standard_normal(out[name].shape)
        drawn = base * np.exp(spread * noise) if base else spread * noise
        out[name] = jnp.asarray(drawn.astype(out[name].dtype))
    for name, factor in factors.items():
        out[name] = (out[name] * factor).astype(out[name].dtype)
    return out
```

```python
from contextlib import ExitStack

import concourse.bass as bass
from concourse import mybir

ALU = mybir.AluOpType
ACT = mybir.ActivationFunctionType
F32 = mybir.dt.float32
F32R = mybir.dt.float32r
U8 = mybir.dt.uint8

P = 128
EPS = 1e-5
CLIP = 100.0
MASKED = -3.0e38
FLOOR = -1.5e38


def gated_xattn_ffn(nc, x, ctx, mask, g_xattn, g_ffn, wq, bq, wk, bk, wo, bo, w_ffn, scale_ffn, bias_ffn, out):
    B, S, D = x.shape
    assert S == P and ctx.shape[1] == P
    DC = D // P
    GB = 2
    G = B // GB
    T = GB * P
    x_rows = x.rearrange("b s d -> s b d")
    ctx_rows = ctx.rearrange("b s d -> s b d")
    out_rows = out.rearrange("b s d -> s b d")

    with ExitStack() as stack:
        def sb(name, shape, dt=F32):
            return stack.enter_context(nc.sbuf_tensor(name, shape, dt))

        def sem(name):
            return stack.enter_context(nc.semaphore(name))

        def bank(name):
            return stack.enter_context(nc.psum_tensor(name, [P, 512], F32))

        xT_bank, cT_bank, y_bank, z_bank = bank("ps_xT"), bank("ps_cT"), bank("ps_Y"), bank("ps_Z")
        s_bank, o_bank, x1T_bank, f_bank = bank("ps_S"), bank("ps_O"), bank("ps_x1T"), bank("ps_F")
        by_chunk = lambda b: b[:, :].rearrange("p (c t) -> p c t", c=DC)
        by_row = lambda b: b[:, :].rearrange("p (b d) -> p b d", b=GB)
        ps_xT, ps_cT, ps_Y = by_chunk(xT_bank), by_chunk(cT_bank), by_chunk(y_bank)
        ps_x1T, ps_F = by_chunk(x1T_bank), by_chunk(f_bank)
        ps_Z, ps_O, ps_Fr = by_row(z_bank), by_row(o_bank), by_row(f_bank)
        ps_S = s_bank[:, 0:GB * P].rearrange("p (b k) -> p b k", b=GB)
        ps_PT = s_bank[:, GB * P:2 * GB * P].rearrange("p (b q) -> p b q", b=GB)
        ps_r = xT_bank[:, 0:GB]

        x_sb, ctx_sb = sb("x_sb", [P, B, D]), sb("ctx_sb", [P, B, D])
        xb_sb = sb("xb_sb", [P, B, D])
        x1_sb = sb("x1_sb", [P, B, D])
        out_sb = sb("out_sb", [P, B, D])
        mask_u8, mask_add = sb("mask_u8", [P, B, P], U8), sb("mask_add", [P, B, P])
        bn_x, bn_1 = sb("bn_x", [P, B, 6]), sb("bn_1", [P, B, 6])
        mv_x, mv_1 = sb("mv_x", [P, B, 2]), sb("mv_1", [P, B, 2])
        ve_x, ve_1 = sb("ve_x", [P, B]), sb("ve_1", [P, B])
        rstd_x, rstd_1 = sb("rstd_x", [P, B]), sb("rstd_1", [P, B])
        mr_x, mr_1 = sb("mr_x", [P, B]), sb("mr_1", [P, B])
        nmr_x, nmr_1 = sb("nmr_x", [P, B]), sb("nmr_1", [P, B])
        r_sb, smax, smax_r, shift = sb("r_sb", [P, B]), sb("smax", [P, B]), sb("smax_r", [P, B]), sb("shift", [P, B])
        psum_p, recip_p = sb("psum_p", [P, B]), sb("recip_p", [P, B])
        xn = sb("xn", [P, 2, GB, D])
        xT = sb("xT", [P, 2, DC, T])
        cT_hi, cT_lo = sb("cT_hi", [P, 2, DC, T], F32R), sb("cT_lo", [P, 2, DC, T], F32R)
        Y_hi, Y_lo = sb("Y_hi", [P, 2, DC, T], F32R), sb("Y_lo", [P, 2, DC, T], F32R)
        Z_sb = sb("Z_sb", [P, 2, GB, D])
        t_sb, p_sb, PT_sb = sb("t_sb", [P, 2, GB, P]), sb("p_sb", [P, 2, GB, P]), sb("PT_sb", [P, 2, GB, P])
        x1n = sb("x1n", [P, 2, GB, D])
        x1T_hi, x1T_lo = sb("x1T_hi", [P, 2, DC, T], F32R), sb("x1T_lo", [P, 2, DC, T], F32R)
        f_sb, f_clip = sb("f_sb", [P, 2, DC, T]), sb("f_clip", [P, 2, DC, T])
        wq_sb, wk_sb, wo_sb = sb("wq_sb", [P, DC, D]), sb("wk_sb", [P, DC, D]), sb("wo_sb", [P, DC, D])
        w_sb, w_sign2 = sb("w_sb", [P, DC, D]), sb("w_sign2", [P, DC, D])
        wqk = sb("wqk", [P, DC, D])
        woT, woT_hi, woT_lo = sb("woT", [P, DC, D]), sb("woT_hi", [P, DC, D], F32R), sb("woT_lo", [P, DC, D], F32R)
        wT = sb("wT", [P, DC, D], F32R)
        vec_rows = sb("vec_rows", [4 * DC, P])
        vec_cols = sb("vec_cols", [P, 4 * DC])
        bq_wide = sb("bq_wide", [P, DC, P])
        derived = sb("derived", [P, 2 * DC + 1])
        bo_sb, bo_g = sb("bo_sb", [P, 1, D]), sb("bo_g", [P, 1, D])
        gates, tanh_g = sb("gates", [P, 2]), sb("tanh_g", [P, 2])
        ident, minus_half = sb("ident", [P, P]), sb("minus_half", [P, GB])
        bqT, bkT, scT, biT = (vec_cols[:, k * DC:(k + 1) * DC] for k in range(4))
        ybias, u, bqbk = derived[:, 0:DC], derived[:, DC:2 * DC], derived[:, 2 * DC:2 * DC + 1]
        ps_vec = o_bank[:, 0:4 * DC]
        ps_derived = o_bank[:, 16:16 + 2 * DC + 1]

        x_loaded, ctx_loaded = [sem(f"x_loaded{g}") for g in range(G)], [sem(f"ctx_loaded{g}") for g in range(G)]
        wqk_loaded, vecs_loaded, wo_loaded, w_loaded = (sem(n) for n in ("wqk_loaded", "vecs_loaded", "wo_loaded", "w_loaded"))
        gates_loaded, bo_loaded, mask_loaded, stored = (sem(n) for n in ("gates_loaded", "bo_loaded", "mask_loaded", "stored"))
        zeroed, ident_ready, half_ready, mask_ready, tanh_ready = (
            sem(n) for n in ("zeroed", "ident_ready", "half_ready", "mask_ready", "tanh_ready"))
        bo_g_ready, sign2_ready, ps_vec_ready, vec_ready, bq_wide_ready = (
            sem(n) for n in ("bo_g_ready", "sign2_ready", "ps_vec_ready", "vec_ready", "bq_wide_ready"))
        ps_wqk_ready, wqk_ready, ps_derived_ready, derived_ready = (
            sem(n) for n in ("ps_wqk_ready", "wqk_ready", "ps_derived_ready", "derived_ready"))
        ps_woT_ready, woT_ready, woT_hi_ready, woT_lo_ready, ps_wT_ready, wT_ready = (
            sem(n) for n in ("ps_woT_ready", "woT_ready", "woT_hi_ready", "woT_lo_ready", "ps_wT_ready", "wT_ready"))
        xT_prod, cT_prod, r_prod, Z_prod, PT_prod, x1T_prod, outT_prod = (
            sem(n) for n in ("xT_prod", "cT_prod", "r_prod", "Z_prod", "PT_prod", "x1T_prod", "outT_prod"))
        Y_prod, S_prod, O_prod, F_prod = (sem(n) for n in ("Y_prod", "S_prod", "O_prod", "F_prod")) 
        bn_x_done, mv_x_done, ve_x_done, rstd_x_done, mr_x_done, nmr_x_done, xn_done = (
            sem(n) for n in ("bn_x_done", "mv_x_done", "ve_x_done", "rstd_x_done", "mr_x_done", "nmr_x_done", "xn_done"))
        bn_1_done, mv_1_done, ve_1_done, rstd_1_done, mr_1_done, nmr_1_done, x1n_done = (
            sem(n) for n in ("bn_1_done", "mv_1_done", "ve_1_done", "rstd_1_done", "mr_1_done", "nmr_1_done", "x1n_done"))
        xb_done, xT_done, cT_hi_done, cT_lo_done, r_done = (
            sem(n) for n in ("xb_done", "xT_done", "cT_hi_done", "cT_lo_done", "r_done"))
        Y_hi_done, Y_lo_done, Z_done, t_done, smax_r_done, shift_done = (
            sem(n) for n in ("Y_hi_done", "Y_lo_done", "Z_done", "t_done", "smax_r_done", "shift_done"))
        p_done, PT_done, recip_done, x1_done = (sem(n) for n in ("p_done", "PT_done", "recip_done", "x1_done"))
        x1T_hi_done, x1T_lo_done, f_done, f_clip_done, out_done = (
            sem(n) for n in ("x1T_hi_done", "x1T_lo_done", "f_done", "f_clip_done", "out_done"))

        rows = lambda g: slice(g * GB, (g + 1) * GB)
        block = stack.enter_context(nc.Block())

        @block.sync
        def _(sp):
            for g in range(G):
                sp.dma_start(x_sb[:, rows(g), :], x_rows[:, rows(g), :]).then_inc(x_loaded[g], 16)
                sp.dma_start(ctx_sb[:, rows(g), :], ctx_rows[:, rows(g), :]).then_inc(ctx_loaded[g], 16)
                if g == 0:
                    sp.dma_start(mask_u8[:], mask.rearrange("(o b) k -> o b k", o=1).to_broadcast([P, B, P])
                                 ).then_inc(mask_loaded, 16)
            for g in range(G):
                sp.wait_ge(out_done, g + 1)
                sp.dma_start(out_rows[:, rows(g), :], out_sb[:, rows(g), :]).then_inc(stored, 16)
            sp.wait_ge(stored, 16 * G)

        @block.scalar
        def _(act):
            act.dma_start(wq_sb[:], wq.rearrange("(c p) d -> p c d", p=P)).then_inc(wqk_loaded, 16)
            act.dma_start(wk_sb[:], wk.rearrange("(c p) d -> p c d", p=P)).then_inc(wqk_loaded, 16)
            for k, v in enumerate((bq, bk, scale_ffn, bias_ffn)):
                act.dma_start(vec_rows[k * DC:(k + 1) * DC, :], v.rearrange("(c p) -> c p", p=P)).then_inc(vecs_loaded, 16)
            for k, v in enumerate((g_xattn, g_ffn)):
                act.dma_start(gates[:, k:k + 1], v.rearrange("(o d) -> o d", o=1).to_broadcast([P, 1])
                              ).then_inc(gates_loaded, 16)
            act.dma_start(wo_sb[:], wo.rearrange("(c p) d -> p c d", p=P)).then_inc(wo_loaded, 16)
            act.dma_start(bo_sb[:, 0, :], bo.rearrange("(o d) -> o d", o=1).to_broadcast([P, D])).then_inc(bo_loaded, 16)
            act.dma_start(w_sb[:], w_ffn.rearrange("(c p) d -> p c d", p=P)).then_inc(w_loaded, 16)
            act.wait_ge(gates_loaded, 32)
            nc.scalar.activation(tanh_g[:], gates[:], ACT.Tanh).then_inc(tanh_ready, 1)

            def setup():
                act.wait_ge(ps_wqk_ready, 1)
                nc.scalar.copy(wqk[:], ps_Y).then_inc(wqk_ready, 1)
                act.wait_ge(ps_woT_ready, 1)
                act.wait_ge(tanh_ready, 1)
                nc.scalar.activation(woT[:], ps_Z, ACT.Identity, scale=tanh_g[:, 0:1]).then_inc(woT_ready, 1)

            def evict_xT(g):
                act.wait_ge(xT_prod, g + 1)
                nc.scalar.copy(xT[:, g % 2], ps_xT).then_inc(xT_done, 1)

            def evict_cT_hi(g):
                act.wait_ge(cT_prod, g + 1)
                nc.scalar.copy(cT_hi[:, g % 2], ps_cT).then_inc(cT_hi_done, 1)

            def evict_x1T_hi(g):
                act.wait_ge(x1T_prod, g + 1)
                nc.scalar.copy(x1T_hi[:, g % 2], ps_x1T).then_inc(x1T_hi_done, 1)

            def evict_Y_hi(g):
                act.wait_ge(Y_prod, g + 1)
                if g == 0:
                    act.wait_ge(derived_ready, 1)
                for c in range(DC):
                    nc.scalar.activation(Y_hi[:, g % 2, c], ps_Y[:, c], ACT.Identity, bias=ybias[:, c:c + 1]
                                         ).then_inc(Y_hi_done, 1)

            def evict_PT(g):
                act.wait_ge(PT_prod, g + 1)
                nc.scalar.copy(PT_sb[:, g % 2], ps_PT).then_inc(PT_done, 1)

            def evict_Z(g):
                act.wait_ge(Z_prod, g + 1)
                nc.scalar.copy(Z_sb[:, g % 2], ps_Z).then_inc(Z_done, 1)

            def exp(g):
                act.wait_ge(shift_done, g + 1)
                for b in range(GB):
                    nc.scalar.activation(p_sb[:, g % 2, b], t_sb[:, g % 2, b], ACT.Exp,
                                         bias=shift[:, g * GB + b:g * GB + b + 1],
                                         accum_out=psum_p[:, g * GB + b:g * GB + b + 1]).then_inc(p_done, 1)

            def ffn_affine(g):
                act.wait_ge(F_prod, g + 1)
                for c in range(DC):
                    nc.scalar.activation(f_sb[:, g % 2, c], ps_F[:, c], ACT.Identity, bias=biT[:, c:c + 1],
                                         scale=scT[:, c:c + 1]).then_inc(f_done, 1)

            setup()
            for i in range(G + 2):
                if i < G:
                    evict_xT(i)
                    evict_cT_hi(i)
                if i >= 2:
                    evict_x1T_hi(i - 2)
                if i < G:
                    evict_Y_hi(i)
                if 1 <= i <= G:
                    evict_PT(i - 1)
                if i >= 2:
                    ffn_affine(i - 2)
                if i < G:
                    evict_Z(i)
                    exp(i)

        @block.gpsimd
        def _(pool):
            nc.gpsimd.memset(ident[:], 0.0).then_inc(zeroed, 1)
            nc.gpsimd.memset(minus_half[:], -0.5).then_inc(half_ready, 1)
            pool.wait_ge(zeroed, 1)
            nc.gpsimd.affine_select(out=ident[:], in_=ident[:], compare_op=ALU.not_equal, fill=1.0, base=0,
                                    pattern=[[-1, P]], channel_multiplier=1).then_inc(ident_ready, 1)

            def layer_norm(g, mv_done, mv, ve, ve_done, rstd, rstd_done, mr, mr_done, nmr, nmr_done, src, dst, done):
                pool.wait_ge(mv_done, GB * (g + 1))
                nc.gpsimd.tensor_scalar(ve[:, rows(g)], mv[:, rows(g), 1], EPS, None, ALU.add).then_inc(ve_done, 1)
                pool.wait_ge(ve_done, g + 1)
                pool.wait_ge(half_ready, 1)
                nc.gpsimd.tensor_tensor(rstd[:, rows(g)], ve[:, rows(g)], minus_half[:], ALU.pow).then_inc(rstd_done, 1)
                pool.wait_ge(rstd_done, g + 1)
                nc.gpsimd.tensor_tensor(mr[:, rows(g)], mv[:, rows(g), 0], rstd[:, rows(g)], ALU.mult).then_inc(mr_done, 1)
                pool.wait_ge(mr_done, g + 1)
                nc.gpsimd.tensor_scalar(nmr[:, rows(g)], mr[:, rows(g)], -1.0, None, ALU.mult).then_inc(nmr_done, 1)
                pool.wait_ge(nmr_done, g + 1)
                for b in range(GB):
                    r = g * GB + b
                    nc.gpsimd.tensor_scalar(dst[:, g % 2, b], src[:, r], rstd[:, r:r + 1], nmr[:, r:r + 1],
                                            ALU.mult, ALU.add).then_inc(done, 1)

            def norm_x(g):
                if g >= 2:
                    pool.wait_ge(xT_prod, g - 1)
                layer_norm(g, mv_x_done, mv_x, ve_x, ve_x_done, rstd_x, rstd_x_done, mr_x, mr_x_done, nmr_x, nmr_x_done,
                           x_sb, xn, xn_done)

            def norm_x1(g):
                if g >= 2:
                    pool.wait_ge(x1T_prod, g - 1)
                layer_norm(g, mv_1_done, mv_1, ve_1, ve_1_done, rstd_1, rstd_1_done, mr_1, mr_1_done, nmr_1, nmr_1_done,
                           x1_sb, x1n, x1n_done)

            def add_bo(g):
                for b in range(GB):
                    r = g * GB + b
                    nc.gpsimd.tensor_tensor(xb_sb[:, r], x_sb[:, r], bo_g[:, 0], ALU.add).then_inc(xb_done, 1)

            def clip(g):
                pool.wait_ge(f_done, DC * (g + 1))
                if g >= 2:
                    pool.wait_ge(outT_prod, g - 1)
                nc.gpsimd.tensor_scalar(f_clip[:, g % 2], f_sb[:, g % 2], CLIP, -CLIP, ALU.min, ALU.max
                                        ).then_inc(f_clip_done, 1)

            norm_x(0)
            pool.wait_ge(mask_loaded, 16)
            nc.gpsimd.tensor_scalar(mask_add[:], mask_u8[:], MASKED, 1.0, ALU.mult, ALU.mult).then_inc(mask_ready, 1)
            pool.wait_ge(w_loaded, 16)
            nc.gpsimd.tensor_scalar(w_sign2[:], w_sb[:], 0.0, 2.0, ALU.is_ge, ALU.mult).then_inc(sign2_ready, 1)
            pool.wait_ge(tanh_ready, 1)
            pool.wait_ge(bo_loaded, 16)
            nc.gpsimd.tensor_scalar(bo_g[:], bo_sb[:], tanh_g[:, 0:1], None, ALU.mult).then_inc(bo_g_ready, 1)
            pool.wait_ge(bo_g_ready, 1)
            for i in range(G + 2):
                if i + 1 < G:
                    norm_x(i + 1)
                if i < G:
                    add_bo(i)
                if i >= 2:
                    clip(i - 2)
                if 1 <= i <= G:
                    norm_x1(i - 1)

        @block.vector
        def _(dve):
            def stats_x(g):
                dve.wait_ge(x_loaded[g], 16)
                for b in range(GB):
                    nc.vector.bn_stats(bn_x[:, g * GB + b], x_sb[:, g * GB + b]).then_inc(bn_x_done, 1)
                for b in range(GB):
                    dve.wait_ge(bn_x_done, GB * g + b + 1)
                    nc.vector.bn_aggr(mv_x[:, g * GB + b], bn_x[:, g * GB + b]).then_inc(mv_x_done, 1)

            def stats_x1(g):
                for b in range(GB):
                    dve.wait_ge(x1_done, GB * g + b + 1)
                    nc.vector.bn_stats(bn_1[:, g * GB + b], x1_sb[:, g * GB + b]).then_inc(bn_1_done, 1)
                for b in range(GB):
                    dve.wait_ge(bn_1_done, GB * g + b + 1)
                    nc.vector.bn_aggr(mv_1[:, g * GB + b], bn_1[:, g * GB + b]).then_inc(mv_1_done, 1)

            def split_cT(g):
                dve.wait_ge(cT_hi_done, g + 1)
                nc.vector.tensor_tensor(cT_lo[:, g % 2], ps_cT, cT_hi[:, g % 2].bitcast(F32), ALU.subtract
                                        ).then_inc(cT_lo_done, 1)

            def split_x1T(g):
                dve.wait_ge(x1T_hi_done, g + 1)
                nc.vector.tensor_tensor(x1T_lo[:, g % 2], ps_x1T, x1T_hi[:, g % 2].bitcast(F32), ALU.subtract
                                        ).then_inc(x1T_lo_done, 1)

            def split_Y(g):
                dve.wait_ge(Y_hi_done, DC * (g + 1))
                for c in range(DC):
                    nc.vector.scalar_tensor_tensor(out=Y_lo[:, g % 2, c], in0=ps_Y[:, c], scalar=ybias[:, c:c + 1],
                                                   in1=Y_hi[:, g % 2, c].bitcast(F32), op0=ALU.add, op1=ALU.subtract
                                                   ).then_inc(Y_lo_done, 1)

            def read_r(g):
                dve.wait_ge(r_prod, g + 1)
                nc.vector.tensor_scalar(r_sb[:, rows(g)], ps_r, bqbk, None, ALU.add).then_inc(r_done, 1)

            def mask_and_max(g):
                dve.wait_ge(S_prod, g + 1)
                for b in range(GB):
                    r = g * GB + b
                    nc.vector.tensor_tensor_reduce(t_sb[:, g % 2, b], ps_S[:, b], mask_add[:, r], 1.0, FLOOR,
                                                   ALU.add, ALU.max, smax[:, r:r + 1]).then_inc(t_done, 1)
                dve.wait_ge(t_done, GB * (g + 1))
                dve.wait_ge(r_done, g + 1)
                nc.vector.tensor_tensor(smax_r[:, rows(g)], smax[:, rows(g)], r_sb[:, rows(g)], ALU.add
                                        ).then_inc(smax_r_done, 1)
                dve.wait_ge(smax_r_done, g + 1)
                nc.vector.tensor_tensor(shift[:, rows(g)], r_sb[:, rows(g)], smax_r[:, rows(g)], ALU.subtract
                                        ).then_inc(shift_done, 1)

            def residual(g):
                dve.wait_ge(p_done, GB * (g + 1))
                nc.vector.reciprocal(recip_p[:, rows(g)], psum_p[:, rows(g)]).then_inc(recip_done, 1)
                dve.wait_ge(recip_done, g + 1)
                dve.wait_ge(xb_done, GB * (g + 1))
                dve.wait_ge(O_prod, g + 1)
                for b in range(GB):
                    r = g * GB + b
                    nc.vector.scalar_tensor_tensor(out=x1_sb[:, r], in0=ps_O[:, b], scalar=recip_p[:, r:r + 1],
                                                   in1=xb_sb[:, r], op0=ALU.mult, op1=ALU.add).then_inc(x1_done, 1)

            def final(g):
                dve.wait_ge(outT_prod, g + 1)
                nc.vector.scalar_tensor_tensor(out=out_sb[:, rows(g)], in0=ps_Fr, scalar=tanh_g[:, 1:2],
                                               in1=x1_sb[:, rows(g)], op0=ALU.mult, op1=ALU.add).then_inc(out_done, 1)

            stats_x(0)
            dve.wait_ge(ps_vec_ready, 1)
            nc.vector.tensor_copy(vec_cols[:], ps_vec).then_inc(vec_ready, 1)
            dve.wait_ge(vec_ready, 1)
            for c in range(DC):
                nc.vector.tensor_copy(bq_wide[:, c], bqT[:, c:c + 1].to_broadcast([P, P])).then_inc(bq_wide_ready, 1)
            dve.wait_ge(ps_derived_ready, 1)
            nc.vector.tensor_copy(derived[:], ps_derived).then_inc(derived_ready, 1)
            dve.wait_ge(woT_ready, 1)
            nc.vector.tensor_copy(woT_hi[:], woT[:]).then_inc(woT_hi_ready, 1)
            dve.wait_ge(woT_hi_ready, 1)
            nc.vector.tensor_tensor(woT_lo[:], woT[:], woT_hi[:].bitcast(F32), ALU.subtract).then_inc(woT_lo_ready, 1)
            dve.wait_ge(derived_ready, 1)
            dve.wait_ge(mask_ready, 1)
            for i in range(G + 2):
                if i + 1 < G:
                    stats_x(i + 1)
                if i < G:
                    split_cT(i)
                if i == 0:
                    dve.wait_ge(ps_wT_ready, 1)
                    nc.vector.tensor_scalar(wT[:], ps_F, 1.0, None, ALU.subtract).then_inc(wT_ready, 1)
                if i >= 2:
                    split_x1T(i - 2)
                if i < G:
                    read_r(i)
                    split_Y(i)
                if 1 <= i <= G:
                    residual(i - 1)
                    stats_x1(i - 1)
                if i < G:
                    mask_and_max(i)
                if i >= 2:
                    final(i - 2)

        @block.tensor
        def _(pe):
            def transposes(dst, src):
                for b in range(GB):
                    for c in range(DC):
                        last = nc.tensor.transpose(dst[:, c, b * P:(b + 1) * P], src[:, b, c * P:(c + 1) * P], ident[:])
                return last

            def split_matmuls(dst, pairs):
                for n, (lhsT, rhs) in enumerate(pairs):
                    last = nc.tensor.matmul(dst, lhsT, rhs, start=(n == 0), stop=(n == len(pairs) - 1))
                return last

            def transpose_x(g):
                pe.wait_ge(xn_done, GB * (g + 1))
                if g >= 1:
                    pe.wait_ge(xT_done, g)
                    pe.wait_ge(r_done, g)
                transposes(ps_xT, xn[:, g % 2]).then_inc(xT_prod, 1)

            def transpose_ctx(g):
                pe.wait_ge(ctx_loaded[g], 16)
                if g >= 1:
                    pe.wait_ge(cT_lo_done, g)
                transposes(ps_cT, ctx_sb[:, rows(g)]).then_inc(cT_prod, 1)

            def transpose_x1(g):
                pe.wait_ge(x1n_done, GB * (g + 1))
                if g >= 1:
                    pe.wait_ge(x1T_lo_done, g)
                transposes(ps_x1T, x1n[:, g % 2]).then_inc(x1T_prod, 1)

            def project_Y(g):
                pe.wait_ge(xT_done, g + 1)
                if g >= 1:
                    pe.wait_ge(Y_lo_done, DC * g)
                else:
                    pe.wait_ge(wqk_ready, 1)
                for m in range(DC):
                    last = split_matmuls(ps_Y[:, m], [(wqk[:, c, m * P:(m + 1) * P], xT[:, g % 2, c]) for c in range(DC)])
                last.then_inc(Y_prod, 1)

            def project_r(g):
                pe.wait_ge(xT_done, g + 1)
                if g == 0:
                    pe.wait_ge(derived_ready, 1)
                for b in range(GB):
                    last = split_matmuls(ps_r[:, b:b + 1], [(xT[:, g % 2, c, b * P:(b + 1) * P], u[:, c:c + 1])
                                                            for c in range(DC)])
                last.then_inc(r_prod, 1)

            def project_Z(g):
                pe.wait_ge(cT_lo_done, g + 1)
                if g >= 1:
                    pe.wait_ge(Z_done, g)
                else:
                    pe.wait_ge(woT_lo_ready, 1)
                for b in range(GB):
                    pairs = []
                    for c in range(DC):
                        hi, lo = (t[:, g % 2, c, b * P:(b + 1) * P] for t in (cT_hi, cT_lo))
                        pairs += [(hi, woT_hi[:, c]), (hi, woT_lo[:, c]), (lo, woT_hi[:, c])]
                    last = split_matmuls(ps_Z[:, b], pairs)
                last.then_inc(Z_prod, 1)

            def scores(g):
                pe.wait_ge(Y_lo_done, DC * (g + 1))
                if g >= 1:
                    pe.wait_ge(PT_done, g)
                for b in range(GB):
                    pairs = []
                    for c in range(DC):
                        y_hi, y_lo, c_hi, c_lo = (t[:, g % 2, c, b * P:(b + 1) * P] for t in (Y_hi, Y_lo, cT_hi, cT_lo))
                        pairs += [(y_hi, c_hi), (y_hi, c_lo), (y_lo, c_hi)]
                    last = split_matmuls(ps_S[:, b], pairs)
                last.then_inc(S_prod, 1)

            def transpose_p(g):
                pe.wait_ge(p_done, GB * (g + 1))
                if g >= 1:
                    pe.wait_ge(PT_done, g)
                for b in range(GB):
                    last = nc.tensor.transpose(ps_PT[:, b], p_sb[:, g % 2, b], ident[:])
                last.then_inc(PT_prod, 1)

            def attend(g):
                pe.wait_ge(PT_done, g + 1)
                pe.wait_ge(Z_done, g + 1)
                if g >= 1:
                    pe.wait_ge(x1_done, GB * g)
                for b in range(GB):
                    last = nc.tensor.matmul(ps_O[:, b], PT_sb[:, g % 2, b], Z_sb[:, g % 2, b], start=True, stop=True)
                last.then_inc(O_prod, 1)

            def ffn(g):
                pe.wait_ge(x1T_lo_done, g + 1)
                if g >= 1:
                    pe.wait_ge(out_done, g)
                else:
                    pe.wait_ge(wT_ready, 1)
                for m in range(DC):
                    pairs = []
                    for c in range(DC):
                        pairs += [(wT[:, c, m * P:(m + 1) * P], t[:, g % 2, c]) for t in (x1T_hi, x1T_lo)]
                    last = split_matmuls(ps_F[:, m], pairs)
                last.then_inc(F_prod, 1)

            def transpose_out(g):
                pe.wait_ge(f_clip_done, g + 1)
                for b in range(GB):
                    for c in range(DC):
                        last = nc.tensor.transpose(ps_Fr[:, b, c * P:(c + 1) * P], f_clip[:, g % 2, c, b * P:(b + 1) * P],
                                                   ident[:])
                last.then_inc(outT_prod, 1)

            pe.wait_ge(ident_ready, 1)
            pe.wait_ge(vecs_loaded, 16 * 4)
            nc.tensor.transpose(ps_vec, vec_rows[:], ident[0:4 * DC, 0:4 * DC]).then_inc(ps_vec_ready, 1)
            transpose_ctx(0)
            pe.wait_ge(wqk_loaded, 32)
            for m in range(DC):
                last = split_matmuls(ps_Y[:, m], [(wq_sb[:, e, m * P:(m + 1) * P], wk_sb[:, e]) for e in range(DC)])
            last.then_inc(ps_wqk_ready, 1)
            pe.wait_ge(wo_loaded, 16)
            transposes(ps_Z, wo_sb).then_inc(ps_woT_ready, 1)
            pe.wait_ge(bq_wide_ready, DC)
            for m in range(DC):
                split_matmuls(ps_derived[:, m:m + 1], [(wk_sb[:, e, m * P:(m + 1) * P], bqT[:, e:e + 1]) for e in range(DC)])
            for m in range(DC):
                split_matmuls(ps_derived[:, DC + m:DC + m + 1],
                              [(wq_sb[:, e, m * P:(m + 1) * P], bkT[:, e:e + 1]) for e in range(DC)])
            split_matmuls(ps_derived[:, 2 * DC:2 * DC + 1], [(bq_wide[:, e], bkT[:, e:e + 1]) for e in range(DC)]
                          ).then_inc(ps_derived_ready, 1)
            for i in range(G + 2):
                if i < G:
                    transpose_x(i)
                    if i > 0:
                        transpose_ctx(i)
                if i == 0:
                    pe.wait_ge(sign2_ready, 1)
                    transposes(ps_F, w_sign2).then_inc(ps_wT_ready, 1)
                if i >= 2:
                    transpose_x1(i - 2)
                if i < G:
                    project_r(i)
                    project_Y(i)
                if 1 <= i <= G:
                    transpose_p(i - 1)
                if i >= 2:
                    ffn(i - 2)
                if i < G:
                    project_Z(i)
                if 1 <= i <= G:
                    attend(i - 1)
                if i < G:
                    scores(i)
                if i >= 2:
                    transpose_out(i - 2)


_INS = ['x', 'ctx_1024', 'mask_BxS2_bk0', 'g_xattn', 'g_ffn', 'L0_xattn_Wq', 'L0_xattn_bq', 'L0_xattn_Wk', 'L0_xattn_bk',
        'L0_xattn_Wo', 'L0_xattn_bo', 'L0_ffn_weights', 'L0_ffn_scale', 'L0_ffn_bias']
_OUTS = [((16, 128, 256), 'float32')]


def kernel(**inputs):
    import numpy as _np
    import concourse.bacc as _bacc
    from concourse import mybir as _mybir
    from concourse.bass_utils import run_bass_kernel_spmd as _run

    nc = _bacc.Bacc("TRN2", target_bir_lowering=False, num_devices=1)
    arrays, args = {}, []
    for name in _INS:
        a = _np.ascontiguousarray(inputs[name])
        arrays[f"in_{name}_dram"] = a
        args.append(nc.dram_tensor(f"in_{name}_dram", a.shape, _mybir.dt.from_np(a.dtype), kind="ExternalInput").ap())
    for i, (shape, dtype) in enumerate(_OUTS):
        dt = _mybir.dt.from_np(_np.dtype(dtype))
        args.append(nc.dram_tensor(f"out_{i}_dram", shape, dt, kind="ExternalOutput").ap())
    gated_xattn_ffn(nc, *args)
    r = _run(nc, [arrays], core_ids=[0])
    got = tuple(r.results[0][f"out_{i}_dram"] for i in range(len(_OUTS)))
    return got[0]
```

```python
from contextlib import ExitStack

import concourse.bass as bass
from concourse import mybir

ALU = mybir.AluOpType
ACT = mybir.ActivationFunctionType
F32 = mybir.dt.float32
F32R = mybir.dt.float32r
U8 = mybir.dt.uint8

P = 128
EPS = 1e-5
CLIP = 100.0
MASKED = -3.0e38
FLOOR = -1.5e38


def gated_xattn_ffn(nc, x, ctx, mask, g_xattn, g_ffn, wq, bq, wk, bk, wo, bo, w_ffn, scale_ffn, bias_ffn, out):
    B, S, D = x.shape
    assert S == P and ctx.shape[1] == P
    DC = D // P
    GB = 2
    G = B // GB
    T = GB * P
    x_rows = x.rearrange("b s d -> s b d")
    ctx_rows = ctx.rearrange("b s d -> s b d")
    out_rows = out.rearrange("b s d -> s b d")

    with ExitStack() as stack:
        def sb(name, shape, dt=F32):
            return stack.enter_context(nc.sbuf_tensor(name, shape, dt))

        def sem(name):
            return stack.enter_context(nc.semaphore(name))

        def bank(name):
            return stack.enter_context(nc.psum_tensor(name, [P, 512], F32))

        xT_bank, cT_bank, y_bank, z_bank = bank("ps_xT"), bank("ps_cT"), bank("ps_Y"), bank("ps_Z")
        s_bank, o_bank, x1T_bank, f_bank = bank("ps_S"), bank("ps_O"), bank("ps_x1T"), bank("ps_F")
        by_chunk = lambda b: b[:, :].rearrange("p (c t) -> p c t", c=DC)
        by_row = lambda b: b[:, :].rearrange("p (b d) -> p b d", b=GB)
        ps_xT, ps_cT, ps_Y = by_chunk(xT_bank), by_chunk(cT_bank), by_chunk(y_bank)
        ps_x1T, ps_F = by_chunk(x1T_bank), by_chunk(f_bank)
        ps_Z, ps_O, ps_Fr = by_row(z_bank), by_row(o_bank), by_row(f_bank)
        ps_S = s_bank[:, 0:GB * P].rearrange("p (b k) -> p b k", b=GB)
        ps_PT = s_bank[:, GB * P:2 * GB * P].rearrange("p (b q) -> p b q", b=GB)

        x_sb, ctx_sb = sb("x_sb", [P, B, D]), sb("ctx_sb", [P, B, D])
        xb_sb = sb("xb_sb", [P, B, D])
        x1_sb = sb("x1_sb", [P, B, D])
        out_sb = sb("out_sb", [P, B, D])
        mask_u8, mask_add = sb("mask_u8", [P, B, P], U8), sb("mask_add", [P, B, P])
        bn_x, bn_1 = sb("bn_x", [P, B, 6]), sb("bn_1", [P, B, 6])
        mv_x, mv_1 = sb("mv_x", [P, B, 2]), sb("mv_1", [P, B, 2])
        ve_x, ve_1 = sb("ve_x", [P, B]), sb("ve_1", [P, B])
        rstd_x, rstd_1 = sb("rstd_x", [P, B]), sb("rstd_1", [P, B])
        mr_x, nmr_x = sb("mr_x", [P, B]), sb("nmr_x", [P, B])
        r_sb, smax, smax_r, shift = sb("r_sb", [P, B]), sb("smax", [P, B]), sb("smax_r", [P, B]), sb("shift", [P, B])
        psum_p, recip_p = sb("psum_p", [P, B]), sb("recip_p", [P, B])
        xn, x_dot_u = sb("xn", [P, 2, GB, D]), sb("x_dot_u", [P, 2, GB, D])
        xT_hi, xT_lo = sb("xT_hi", [P, 2, DC, T], F32R), sb("xT_lo", [P, 2, DC, T], F32R)
        cT = sb("cT", [P, 2, DC, T])
        Y_sb = sb("Y_sb", [P, 2, DC, T])
        Z_sb = sb("Z_sb", [P, 2, GB, D])
        t_sb, p_sb, PT_sb = sb("t_sb", [P, 2, GB, P]), sb("p_sb", [P, 2, GB, P]), sb("PT_sb", [P, 2, GB, P])
        x1n = sb("x1n", [P, 2, GB, D])
        x1T_hi, x1T_lo = sb("x1T_hi", [P, 2, DC, T], F32R), sb("x1T_lo", [P, 2, DC, T], F32R)
        f_sb, f_clip = sb("f_sb", [P, 2, DC, T]), sb("f_clip", [P, 2, DC, T])
        wq_sb, wk_sb, wo_sb = sb("wq_sb", [P, DC, D]), sb("wk_sb", [P, DC, D]), sb("wo_sb", [P, DC, D])
        w_sb, w_sign2 = sb("w_sb", [P, DC, D]), sb("w_sign2", [P, DC, D])
        wqk_hi, wqk_lo = sb("wqk_hi", [P, DC, D], F32R), sb("wqk_lo", [P, DC, D], F32R)
        woT = sb("woT", [P, DC, D])
        wT = sb("wT", [P, DC, D], F32R)
        vec_rows = sb("vec_rows", [4 * DC, P])
        vec_cols = sb("vec_cols", [P, 4 * DC])
        bk_wide = sb("bk_wide", [P, DC, P])
        derived = sb("derived", [P, DC + 1])
        u_wide = sb("u_wide", [P, D])
        bo_sb, bo_g = sb("bo_sb", [P, 1, D]), sb("bo_g", [P, 1, D])
        gates, tanh_g = sb("gates", [P, 2]), sb("tanh_g", [P, 2])
        ident, minus_half = sb("ident", [P, P]), sb("minus_half", [P, GB])
        bqT, bkT, scT, biT = (vec_cols[:, k * DC:(k + 1) * DC] for k in range(4))
        ybias, bqbk = derived[:, 0:DC], derived[:, DC:DC + 1]
        ps_vec = o_bank[:, 0:4 * DC]
        ps_derived, ps_u = o_bank[:, 16:17 + DC], o_bank[:, D:2 * D]

        x_loaded, ctx_loaded = [sem(f"x_loaded{g}") for g in range(G)], [sem(f"ctx_loaded{g}") for g in range(G)]
        wqk_loaded, vecs_loaded, wo_loaded, w_loaded = (sem(n) for n in ("wqk_loaded", "vecs_loaded", "wo_loaded", "w_loaded"))
        gates_loaded, bo_loaded, mask_loaded, stored = (sem(n) for n in ("gates_loaded", "bo_loaded", "mask_loaded", "stored"))
        zeroed, ident_ready, half_ready, mask_ready, tanh_ready = (
            sem(n) for n in ("zeroed", "ident_ready", "half_ready", "mask_ready", "tanh_ready"))
        bo_g_ready, sign2_ready, ps_vec_ready, vec_ready, bk_wide_ready = (
            sem(n) for n in ("bo_g_ready", "sign2_ready", "ps_vec_ready", "vec_ready", "bk_wide_ready"))
        ps_wqk_ready, wqk_ready, ps_derived_ready, derived_ready = (
            sem(n) for n in ("ps_wqk_ready", "wqk_ready", "ps_derived_ready", "derived_ready"))
        ps_woT_ready, woT_ready, wqk_lo_ready, u_ready, ps_wT_ready, wT_ready = (
            sem(n) for n in ("ps_woT_ready", "woT_ready", "wqk_lo_ready", "u_ready", "ps_wT_ready", "wT_ready"))
        xT_prod, cT_prod, Z_prod, PT_prod, x1T_prod, outT_prod = (
            sem(n) for n in ("xT_prod", "cT_prod", "Z_prod", "PT_prod", "x1T_prod", "outT_prod"))
        Y_prod, S_prod, O_prod, F_prod = (sem(n) for n in ("Y_prod", "S_prod", "O_prod", "F_prod")) 
        bn_x_done, mv_x_done, ve_x_done, rstd_x_done, mr_x_done, nmr_x_done, xn_done = (
            sem(n) for n in ("bn_x_done", "mv_x_done", "ve_x_done", "rstd_x_done", "mr_x_done", "nmr_x_done", "xn_done"))
        bn_1_done, mv_1_done, ve_1_done, rstd_1_done, x1n_done = (
            sem(n) for n in ("bn_1_done", "mv_1_done", "ve_1_done", "rstd_1_done", "x1n_done"))
        xb_done, xT_hi_done, xT_lo_done, cT_done, r_done = (
            sem(n) for n in ("xb_done", "xT_hi_done", "xT_lo_done", "cT_done", "r_done"))
        Y_done, Z_done, t_done, smax_r_done, shift_done = (
            sem(n) for n in ("Y_done", "Z_done", "t_done", "smax_r_done", "shift_done"))
        p_done, PT_done, recip_done, x1_done = (sem(n) for n in ("p_done", "PT_done", "recip_done", "x1_done"))
        x1T_hi_done, x1T_lo_done, f_done, f_clip_done, out_done = (
            sem(n) for n in ("x1T_hi_done", "x1T_lo_done", "f_done", "f_clip_done", "out_done"))

        rows = lambda g: slice(g * GB, (g + 1) * GB)
        block = stack.enter_context(nc.Block())

        @block.sync
        def _(sp):
            for g in range(G):
                sp.dma_start(x_sb[:, rows(g), :], x_rows[:, rows(g), :]).then_inc(x_loaded[g], 16)
                sp.dma_start(ctx_sb[:, rows(g), :], ctx_rows[:, rows(g), :]).then_inc(ctx_loaded[g], 16)
                if g == 0:
                    sp.dma_start(mask_u8[:], mask.rearrange("(o b) k -> o b k", o=1).to_broadcast([P, B, P])
                                 ).then_inc(mask_loaded, 16)
            for g in range(G):
                sp.wait_ge(out_done, g + 1)
                sp.dma_start(out_rows[:, rows(g), :], out_sb[:, rows(g), :]).then_inc(stored, 16)
            sp.wait_ge(stored, 16 * G)

        @block.scalar
        def _(act):
            act.dma_start(wq_sb[:], wq.rearrange("(c p) d -> p c d", p=P)).then_inc(wqk_loaded, 16)
            act.dma_start(wk_sb[:], wk.rearrange("(c p) d -> p c d", p=P)).then_inc(wqk_loaded, 16)
            for k, v in enumerate((bq, bk, scale_ffn, bias_ffn)):
                act.dma_start(vec_rows[k * DC:(k + 1) * DC, :], v.rearrange("(c p) -> c p", p=P)).then_inc(vecs_loaded, 16)
            for k, v in enumerate((g_xattn, g_ffn)):
                act.dma_start(gates[:, k:k + 1], v.rearrange("(o d) -> o d", o=1).to_broadcast([P, 1])
                              ).then_inc(gates_loaded, 16)
            act.dma_start(wo_sb[:], wo.rearrange("(c p) d -> p c d", p=P)).then_inc(wo_loaded, 16)
            act.dma_start(bo_sb[:, 0, :], bo.rearrange("(o d) -> o d", o=1).to_broadcast([P, D])).then_inc(bo_loaded, 16)
            act.dma_start(w_sb[:], w_ffn.rearrange("(c p) d -> p c d", p=P)).then_inc(w_loaded, 16)
            act.wait_ge(gates_loaded, 32)
            nc.scalar.activation(tanh_g[:], gates[:], ACT.Tanh).then_inc(tanh_ready, 1)

            def setup():
                act.wait_ge(ps_wqk_ready, 1)
                nc.scalar.copy(wqk_hi[:], ps_Y).then_inc(wqk_ready, 1)
                act.wait_ge(ps_woT_ready, 1)
                nc.scalar.activation(woT[:], ps_Z, ACT.Identity, scale=tanh_g[:, 0:1]).then_inc(woT_ready, 1)

            def evict_xT_hi(g):
                act.wait_ge(xT_prod, g + 1)
                nc.scalar.copy(xT_hi[:, g % 2], ps_xT).then_inc(xT_hi_done, 1)

            def evict_cT(g):
                act.wait_ge(cT_prod, g + 1)
                nc.scalar.copy(cT[:, g % 2], ps_cT).then_inc(cT_done, 1)

            def evict_x1T_hi(g):
                act.wait_ge(x1T_prod, g + 1)
                nc.scalar.copy(x1T_hi[:, g % 2], ps_x1T).then_inc(x1T_hi_done, 1)

            def evict_Y(g):
                act.wait_ge(Y_prod, g + 1)
                if g == 0:
                    act.wait_ge(derived_ready, 1)
                for c in range(DC):
                    nc.scalar.activation(Y_sb[:, g % 2, c], ps_Y[:, c], ACT.Identity, bias=ybias[:, c:c + 1]
                                         ).then_inc(Y_done, 1)

            def evict_PT(g):
                act.wait_ge(PT_prod, g + 1)
                nc.scalar.copy(PT_sb[:, g % 2], ps_PT).then_inc(PT_done, 1)

            def evict_Z(g):
                act.wait_ge(Z_prod, g + 1)
                nc.scalar.copy(Z_sb[:, g % 2], ps_Z).then_inc(Z_done, 1)

            def exp(g):
                act.wait_ge(shift_done, g + 1)
                for b in range(GB):
                    nc.scalar.activation(p_sb[:, g % 2, b], t_sb[:, g % 2, b], ACT.Exp,
                                         bias=shift[:, g * GB + b:g * GB + b + 1],
                                         accum_out=psum_p[:, g * GB + b:g * GB + b + 1]).then_inc(p_done, 1)

            def ffn_affine(g):
                act.wait_ge(F_prod, g + 1)
                for c in range(DC):
                    nc.scalar.activation(f_sb[:, g % 2, c], ps_F[:, c], ACT.Identity, bias=biT[:, c:c + 1],
                                         scale=scT[:, c:c + 1]).then_inc(f_done, 1)

            act.wait_ge(tanh_ready, 1)
            setup()
            for i in range(G + 2):
                if i >= 2:
                    evict_x1T_hi(i - 2)
                if 1 <= i <= G:
                    evict_PT(i - 1)
                if i < G:
                    evict_xT_hi(i)
                    evict_cT(i)
                    evict_Y(i)
                if i >= 2:
                    ffn_affine(i - 2)
                if i < G:
                    exp(i)
                    evict_Z(i)

        @block.gpsimd
        def _(pool):
            nc.gpsimd.memset(ident[:], 0.0).then_inc(zeroed, 1)
            nc.gpsimd.memset(minus_half[:], -0.5).then_inc(half_ready, 1)
            pool.wait_ge(zeroed, 1)
            nc.gpsimd.affine_select(out=ident[:], in_=ident[:], compare_op=ALU.not_equal, fill=1.0, base=0,
                                    pattern=[[-1, P]], channel_multiplier=1).then_inc(ident_ready, 1)

            def rstd_1s(g):
                pool.wait_ge(ve_1_done, g + 1)
                nc.gpsimd.tensor_tensor(rstd_1[:, rows(g)], ve_1[:, rows(g)], minus_half[:], ALU.pow).then_inc(rstd_1_done, 1)

            def norm_x(g):
                pool.wait_ge(ve_x_done, g + 1)
                nc.gpsimd.tensor_tensor(rstd_x[:, rows(g)], ve_x[:, rows(g)], minus_half[:], ALU.pow).then_inc(rstd_x_done, 1)
                pool.wait_ge(rstd_x_done, g + 1)
                nc.gpsimd.tensor_tensor(mr_x[:, rows(g)], mv_x[:, rows(g), 0], rstd_x[:, rows(g)], ALU.mult).then_inc(mr_x_done, 1)
                pool.wait_ge(mr_x_done, g + 1)
                nc.gpsimd.tensor_scalar(nmr_x[:, rows(g)], mr_x[:, rows(g)], -1.0, None, ALU.mult).then_inc(nmr_x_done, 1)
                pool.wait_ge(nmr_x_done, g + 1)
                if g >= 2:
                    pool.wait_ge(xT_prod, g - 1)
                    pool.wait_ge(r_done, GB * (g - 1))
                for b in range(GB):
                    r = g * GB + b
                    nc.gpsimd.tensor_scalar(xn[:, g % 2, b], x_sb[:, r], rstd_x[:, r:r + 1], nmr_x[:, r:r + 1],
                                            ALU.mult, ALU.add).then_inc(xn_done, 1)

            def add_bo(g):
                for b in range(GB):
                    r = g * GB + b
                    nc.gpsimd.tensor_tensor(xb_sb[:, r], x_sb[:, r], bo_g[:, 0], ALU.add).then_inc(xb_done, 1)

            pool.wait_ge(half_ready, 1)
            norm_x(0)
            pool.wait_ge(mask_loaded, 16)
            nc.gpsimd.tensor_scalar(mask_add[:], mask_u8[:], MASKED, 1.0, ALU.mult, ALU.mult).then_inc(mask_ready, 1)
            pool.wait_ge(w_loaded, 16)
            nc.gpsimd.tensor_scalar(w_sign2[:], w_sb[:], 0.0, 2.0, ALU.is_ge, ALU.mult).then_inc(sign2_ready, 1)
            pool.wait_ge(tanh_ready, 1)
            pool.wait_ge(bo_loaded, 16)
            nc.gpsimd.tensor_scalar(bo_g[:], bo_sb[:], tanh_g[:, 0:1], None, ALU.mult).then_inc(bo_g_ready, 1)
            pool.wait_ge(bo_g_ready, 1)
            for i in range(G + 1):
                if i >= 1:
                    rstd_1s(i - 1)
                if i + 1 < G:
                    norm_x(i + 1)
                if i < G:
                    add_bo(i)

        @block.vector
        def _(dve):
            def stats_x(g):
                dve.wait_ge(x_loaded[g], 16)
                for b in range(GB):
                    nc.vector.bn_stats(bn_x[:, g * GB + b], x_sb[:, g * GB + b]).then_inc(bn_x_done, 1)
                for b in range(GB):
                    dve.wait_ge(bn_x_done, GB * g + b + 1)
                    nc.vector.bn_aggr(mv_x[:, g * GB + b], bn_x[:, g * GB + b]).then_inc(mv_x_done, 1)
                dve.wait_ge(mv_x_done, GB * (g + 1))
                nc.vector.tensor_scalar(ve_x[:, rows(g)], mv_x[:, rows(g), 1], EPS, None, ALU.add).then_inc(ve_x_done, 1)

            def stats_x1(g):
                for b in range(GB):
                    dve.wait_ge(x1_done, GB * g + b + 1)
                    nc.vector.bn_stats(bn_1[:, g * GB + b], x1_sb[:, g * GB + b]).then_inc(bn_1_done, 1)
                for b in range(GB):
                    dve.wait_ge(bn_1_done, GB * g + b + 1)
                    nc.vector.bn_aggr(mv_1[:, g * GB + b], bn_1[:, g * GB + b]).then_inc(mv_1_done, 1)
                dve.wait_ge(mv_1_done, GB * (g + 1))
                nc.vector.tensor_scalar(ve_1[:, rows(g)], mv_1[:, rows(g), 1], EPS, None, ALU.add).then_inc(ve_1_done, 1)

            def split_xT(g):
                dve.wait_ge(xT_hi_done, g + 1)
                nc.vector.tensor_tensor(xT_lo[:, g % 2], ps_xT, xT_hi[:, g % 2].bitcast(F32), ALU.subtract
                                        ).then_inc(xT_lo_done, 1)

            def split_x1T(g):
                dve.wait_ge(x1T_hi_done, g + 1)
                nc.vector.tensor_tensor(x1T_lo[:, g % 2], ps_x1T, x1T_hi[:, g % 2].bitcast(F32), ALU.subtract
                                        ).then_inc(x1T_lo_done, 1)

            def norm_x1(g):
                dve.wait_ge(rstd_1_done, g + 1)
                for b in range(GB):
                    r = g * GB + b
                    nc.vector.tensor_scalar(x1n[:, g % 2, b], x1_sb[:, r], mv_1[:, r, 0:1], rstd_1[:, r:r + 1],
                                            ALU.subtract, ALU.mult).then_inc(x1n_done, 1)

            def dot_u(g):
                dve.wait_ge(xn_done, GB * (g + 1))
                for b in range(GB):
                    r = g * GB + b
                    nc.vector.tensor_tensor_reduce(x_dot_u[:, g % 2, b], xn[:, g % 2, b], u_wide[:], 1.0, bqbk,
                                                   ALU.mult, ALU.add, r_sb[:, r:r + 1]).then_inc(r_done, 1)

            def clip(g):
                dve.wait_ge(f_done, DC * (g + 1))
                nc.vector.tensor_scalar(f_clip[:, g % 2], f_sb[:, g % 2], CLIP, -CLIP, ALU.min, ALU.max
                                        ).then_inc(f_clip_done, 1)

            def mask_and_max(g):
                dve.wait_ge(S_prod, g + 1)
                for b in range(GB):
                    r = g * GB + b
                    nc.vector.tensor_tensor_reduce(t_sb[:, g % 2, b], ps_S[:, b], mask_add[:, r], 1.0, FLOOR,
                                                   ALU.add, ALU.max, smax[:, r:r + 1]).then_inc(t_done, 1)
                dve.wait_ge(t_done, GB * (g + 1))
                dve.wait_ge(r_done, GB * (g + 1))
                nc.vector.tensor_tensor(smax_r[:, rows(g)], smax[:, rows(g)], r_sb[:, rows(g)], ALU.add
                                        ).then_inc(smax_r_done, 1)
                dve.wait_ge(smax_r_done, g + 1)
                nc.vector.tensor_tensor(shift[:, rows(g)], r_sb[:, rows(g)], smax_r[:, rows(g)], ALU.subtract
                                        ).then_inc(shift_done, 1)

            def residual(g):
                dve.wait_ge(p_done, GB * (g + 1))
                nc.vector.reciprocal(recip_p[:, rows(g)], psum_p[:, rows(g)]).then_inc(recip_done, 1)
                dve.wait_ge(recip_done, g + 1)
                dve.wait_ge(xb_done, GB * (g + 1))
                dve.wait_ge(O_prod, g + 1)
                for b in range(GB):
                    r = g * GB + b
                    nc.vector.scalar_tensor_tensor(out=x1_sb[:, r], in0=ps_O[:, b], scalar=recip_p[:, r:r + 1],
                                                   in1=xb_sb[:, r], op0=ALU.mult, op1=ALU.add).then_inc(x1_done, 1)

            def final(g):
                dve.wait_ge(outT_prod, g + 1)
                nc.vector.scalar_tensor_tensor(out=out_sb[:, rows(g)], in0=ps_Fr, scalar=tanh_g[:, 1:2],
                                               in1=x1_sb[:, rows(g)], op0=ALU.mult, op1=ALU.add).then_inc(out_done, 1)

            stats_x(0)
            dve.wait_ge(ps_vec_ready, 1)
            nc.vector.tensor_copy(vec_cols[:], ps_vec).then_inc(vec_ready, 1)
            dve.wait_ge(vec_ready, 1)
            for c in range(DC):
                nc.vector.tensor_copy(bk_wide[:, c], bkT[:, c:c + 1].to_broadcast([P, P])).then_inc(bk_wide_ready, 1)
            dve.wait_ge(wqk_ready, 1)
            nc.vector.tensor_tensor(wqk_lo[:], ps_Y, wqk_hi[:].bitcast(F32), ALU.subtract).then_inc(wqk_lo_ready, 1)
            dve.wait_ge(ps_derived_ready, 1)
            nc.vector.tensor_copy(derived[:], ps_derived).then_inc(derived_ready, 1)
            nc.vector.tensor_copy(u_wide[:], ps_u).then_inc(u_ready, 1)
            for i in range(G + 2):
                if i >= 2:
                    split_x1T(i - 2)
                if i < G:
                    split_xT(i)
                if i == 0:
                    dve.wait_ge(ps_wT_ready, 1)
                    nc.vector.tensor_scalar(wT[:], ps_F, 1.0, None, ALU.subtract).then_inc(wT_ready, 1)
                    dve.wait_ge(u_ready, 1)
                    dve.wait_ge(mask_ready, 1)
                if 1 <= i <= G:
                    residual(i - 1)
                    stats_x1(i - 1)
                if i + 1 < G:
                    stats_x(i + 1)
                if 1 <= i <= G:
                    norm_x1(i - 1)
                if i < G:
                    dot_u(i)
                if i >= 2:
                    clip(i - 2)
                if i < G:
                    mask_and_max(i)
                if i >= 2:
                    final(i - 2)

        @block.tensor
        def _(pe):
            def transposes(dst, src):
                for b in range(GB):
                    for c in range(DC):
                        last = nc.tensor.transpose(dst[:, c, b * P:(b + 1) * P], src[:, b, c * P:(c + 1) * P], ident[:])
                return last

            def split_matmuls(dst, pairs):
                for n, (lhsT, rhs) in enumerate(pairs):
                    last = nc.tensor.matmul(dst, lhsT, rhs, start=(n == 0), stop=(n == len(pairs) - 1))
                return last

            def transpose_x(g):
                pe.wait_ge(xn_done, GB * (g + 1))
                if g >= 1:
                    pe.wait_ge(xT_lo_done, g)
                transposes(ps_xT, xn[:, g % 2]).then_inc(xT_prod, 1)

            def transpose_ctx(g):
                pe.wait_ge(ctx_loaded[g], 16)
                if g >= 1:
                    pe.wait_ge(cT_done, g)
                transposes(ps_cT, ctx_sb[:, rows(g)]).then_inc(cT_prod, 1)

            def transpose_x1(g):
                pe.wait_ge(x1n_done, GB * (g + 1))
                if g >= 1:
                    pe.wait_ge(x1T_lo_done, g)
                transposes(ps_x1T, x1n[:, g % 2]).then_inc(x1T_prod, 1)

            def project_Y(g):
                pe.wait_ge(xT_lo_done, g + 1)
                if g >= 1:
                    pe.wait_ge(Y_done, DC * g)
                else:
                    pe.wait_ge(wqk_lo_ready, 1)
                for m in range(DC):
                    pairs = []
                    for c in range(DC):
                        w_hi, w_lo = (w[:, c, m * P:(m + 1) * P] for w in (wqk_hi, wqk_lo))
                        pairs += [(w_hi, xT_hi[:, g % 2, c]), (w_hi, xT_lo[:, g % 2, c]), (w_lo, xT_hi[:, g % 2, c])]
                    last = split_matmuls(ps_Y[:, m], pairs)
                last.then_inc(Y_prod, 1)

            def project_Z(g):
                pe.wait_ge(cT_done, g + 1)
                if g >= 1:
                    pe.wait_ge(Z_done, g)
                else:
                    pe.wait_ge(woT_ready, 1)
                for b in range(GB):
                    last = split_matmuls(ps_Z[:, b], [(cT[:, g % 2, c, b * P:(b + 1) * P], woT[:, c]) for c in range(DC)])
                last.then_inc(Z_prod, 1)

            def scores(g):
                pe.wait_ge(Y_done, DC * (g + 1))
                pe.wait_ge(cT_done, g + 1)
                if g >= 1:
                    pe.wait_ge(PT_done, g)
                for b in range(GB):
                    last = split_matmuls(ps_S[:, b], [(Y_sb[:, g % 2, c, b * P:(b + 1) * P], cT[:, g % 2, c, b * P:(b + 1) * P])
                                                      for c in range(DC)])
                last.then_inc(S_prod, 1)

            def transpose_p(g):
                pe.wait_ge(p_done, GB * (g + 1))
                if g >= 1:
                    pe.wait_ge(PT_done, g)
                for b in range(GB):
                    last = nc.tensor.transpose(ps_PT[:, b], p_sb[:, g % 2, b], ident[:])
                last.then_inc(PT_prod, 1)

            def attend(g):
                pe.wait_ge(PT_done, g + 1)
                pe.wait_ge(Z_done, g + 1)
                if g >= 1:
                    pe.wait_ge(x1_done, GB * g)
                for b in range(GB):
                    last = nc.tensor.matmul(ps_O[:, b], PT_sb[:, g % 2, b], Z_sb[:, g % 2, b], start=True, stop=True)
                last.then_inc(O_prod, 1)

            def ffn(g):
                pe.wait_ge(x1T_lo_done, g + 1)
                if g >= 1:
                    pe.wait_ge(out_done, g)
                else:
                    pe.wait_ge(wT_ready, 1)
                for m in range(DC):
                    pairs = []
                    for c in range(DC):
                        pairs += [(wT[:, c, m * P:(m + 1) * P], t[:, g % 2, c]) for t in (x1T_hi, x1T_lo)]
                    last = split_matmuls(ps_F[:, m], pairs)
                last.then_inc(F_prod, 1)

            def transpose_out(g):
                pe.wait_ge(f_clip_done, g + 1)
                for b in range(GB):
                    for c in range(DC):
                        last = nc.tensor.transpose(ps_Fr[:, b, c * P:(c + 1) * P], f_clip[:, g % 2, c, b * P:(b + 1) * P],
                                                   ident[:])
                last.then_inc(outT_prod, 1)

            pe.wait_ge(ident_ready, 1)
            pe.wait_ge(vecs_loaded, 16 * 4)
            nc.tensor.transpose(ps_vec, vec_rows[:], ident[0:4 * DC, 0:4 * DC]).then_inc(ps_vec_ready, 1)
            transpose_ctx(0)
            pe.wait_ge(wqk_loaded, 32)
            for m in range(DC):
                last = split_matmuls(ps_Y[:, m], [(wq_sb[:, e, m * P:(m + 1) * P], wk_sb[:, e]) for e in range(DC)])
            last.then_inc(ps_wqk_ready, 1)
            pe.wait_ge(wo_loaded, 16)
            transposes(ps_Z, wo_sb).then_inc(ps_woT_ready, 1)
            pe.wait_ge(bk_wide_ready, DC)
            for m in range(DC):
                split_matmuls(ps_derived[:, m:m + 1], [(wk_sb[:, e, m * P:(m + 1) * P], bqT[:, e:e + 1]) for e in range(DC)])
            split_matmuls(ps_derived[:, DC:DC + 1], [(bk_wide[:, e], bqT[:, e:e + 1]) for e in range(DC)])
            split_matmuls(ps_u, [(bk_wide[:, e], wq_sb[:, e]) for e in range(DC)]).then_inc(ps_derived_ready, 1)
            for i in range(G + 2):
                if 1 <= i <= G:
                    transpose_p(i - 1)
                if i < G:
                    transpose_x(i)
                if 1 <= i <= G:
                    attend(i - 1)
                if 1 <= i < G:
                    transpose_ctx(i)
                if i == 0:
                    pe.wait_ge(sign2_ready, 1)
                    transposes(ps_F, w_sign2).then_inc(ps_wT_ready, 1)
                if i < G:
                    project_Y(i)
                if i >= 2:
                    ffn(i - 2)
                if i < G:
                    scores(i)
                    project_Z(i)
                if 1 <= i <= G:
                    transpose_x1(i - 1)
                if i >= 2:
                    transpose_out(i - 2)


_INS = ['x', 'ctx_1024', 'mask_BxS2_bk0', 'g_xattn', 'g_ffn', 'L0_xattn_Wq', 'L0_xattn_bq', 'L0_xattn_Wk', 'L0_xattn_bk',
        'L0_xattn_Wo', 'L0_xattn_bo', 'L0_ffn_weights', 'L0_ffn_scale', 'L0_ffn_bias']
_OUTS = [((16, 128, 256), 'float32')]


def kernel(**inputs):
    import numpy as _np
    import concourse.bacc as _bacc
    from concourse import mybir as _mybir
    from concourse.bass_utils import run_bass_kernel_spmd as _run

    nc = _bacc.Bacc("TRN2", target_bir_lowering=False, num_devices=1)
    arrays, args = {}, []
    for name in _INS:
        a = _np.ascontiguousarray(inputs[name])
        arrays[f"in_{name}_dram"] = a
        args.append(nc.dram_tensor(f"in_{name}_dram", a.shape, _mybir.dt.from_np(a.dtype), kind="ExternalInput").ap())
    for i, (shape, dtype) in enumerate(_OUTS):
        dt = _mybir.dt.from_np(_np.dtype(dtype))
        args.append(nc.dram_tensor(f"out_{i}_dram", shape, dt, kind="ExternalOutput").ap())
    gated_xattn_ffn(nc, *args)
    r = _run(nc, [arrays], core_ids=[0])
    got = tuple(r.results[0][f"out_{i}_dram"] for i in range(len(_OUTS)))
    return got[0]
```

```python
from contextlib import ExitStack

import concourse.bass as bass
from concourse import mybir

ALU = mybir.AluOpType
ACT = mybir.ActivationFunctionType
F32 = mybir.dt.float32
F32R = mybir.dt.float32r
U8 = mybir.dt.uint8

P = 128
WARM_UP = 18
EPS = 1e-5
CLIP = 100.0
MASKED = -3.0e38
FLOOR = -1.5e38


def gated_xattn_ffn(nc, x, ctx, mask, g_xattn, g_ffn, wq, bq, wk, bk, wo, bo, w_ffn, scale_ffn, bias_ffn, out):
    B, S, D = x.shape
    assert S == P and ctx.shape[1] == P
    DC = D // P
    GB = 2
    G = B // GB
    T = GB * P
    x_rows = x.rearrange("b s d -> s b d")
    ctx_rows = ctx.rearrange("b s d -> s b d")
    out_rows = out.rearrange("b s d -> s b d")

    with ExitStack() as stack:
        def sb(name, shape, dt=F32):
            return stack.enter_context(nc.sbuf_tensor(name, shape, dt))

        def sem(name):
            return stack.enter_context(nc.semaphore(name))

        def bank(name):
            return stack.enter_context(nc.psum_tensor(name, [P, 512], F32))

        xT_bank, cT_bank, y_bank, z_bank = bank("ps_xT"), bank("ps_cT"), bank("ps_Y"), bank("ps_Z")
        s_bank, o_bank, x1T_bank, f_bank = bank("ps_S"), bank("ps_O"), bank("ps_x1T"), bank("ps_F")
        by_chunk = lambda b: b[:, :].rearrange("p (c t) -> p c t", c=DC)
        by_row = lambda b: b[:, :].rearrange("p (b d) -> p b d", b=GB)
        ps_xT, ps_cT, ps_Y = by_chunk(xT_bank), by_chunk(cT_bank), by_chunk(y_bank)
        ps_x1T, ps_F = by_chunk(x1T_bank), by_chunk(f_bank)
        ps_Z, ps_O, ps_Fr = by_row(z_bank), by_row(o_bank), by_row(f_bank)
        ps_S = s_bank[:, 0:GB * P].rearrange("p (b k) -> p b k", b=GB)
        ps_PT = s_bank[:, GB * P:2 * GB * P].rearrange("p (b q) -> p b q", b=GB)

        x_sb, ctx_sb = sb("x_sb", [P, B, D]), sb("ctx_sb", [P, B, D])
        xb_sb = sb("xb_sb", [P, B, D])
        x1_sb = sb("x1_sb", [P, B, D])
        out_sb = sb("out_sb", [P, B, D])
        mask_u8, mask_add = sb("mask_u8", [P, B, P], U8), sb("mask_add", [P, B, P])
        bn_x, bn_1 = sb("bn_x", [P, B, 6]), sb("bn_1", [P, B, 6])
        mv_x, mv_1 = sb("mv_x", [P, B, 2]), sb("mv_1", [P, B, 2])
        ve_x, ve_1 = sb("ve_x", [P, B]), sb("ve_1", [P, B])
        rstd_x, rstd_1 = sb("rstd_x", [P, B]), sb("rstd_1", [P, B])
        mr_x, nmr_x = sb("mr_x", [P, B]), sb("nmr_x", [P, B])
        r_sb, smax, smax_r, shift = sb("r_sb", [P, B]), sb("smax", [P, B]), sb("smax_r", [P, B]), sb("shift", [P, B])
        psum_p, recip_p = sb("psum_p", [P, B]), sb("recip_p", [P, B])
        xn, x_dot_u = sb("xn", [P, 3, GB, D]), sb("x_dot_u", [P, 2, GB, D])
        xT_hi, xT_lo = sb("xT_hi", [P, 2, DC, T], F32R), sb("xT_lo", [P, 2, DC, T], F32R)
        cT = sb("cT", [P, 2, DC, T])
        Y_sb = sb("Y_sb", [P, 2, DC, T])
        Z_sb = sb("Z_sb", [P, 2, GB, D])
        t_sb, p_sb, PT_sb = sb("t_sb", [P, 2, GB, P]), sb("p_sb", [P, 2, GB, P]), sb("PT_sb", [P, 2, GB, P])
        x1n = sb("x1n", [P, 2, GB, D])
        x1T_hi, x1T_lo = sb("x1T_hi", [P, 2, DC, T], F32R), sb("x1T_lo", [P, 2, DC, T], F32R)
        f_sb, f_clip = sb("f_sb", [P, 2, DC, T]), sb("f_clip", [P, 2, DC, T])
        wq_sb, wk_sb, wo_sb = sb("wq_sb", [P, DC, D]), sb("wk_sb", [P, DC, D]), sb("wo_sb", [P, DC, D])
        w_sb, w_sign2 = sb("w_sb", [P, DC, D]), sb("w_sign2", [P, DC, D])
        wqk_hi, wqk_lo = sb("wqk_hi", [P, DC, D], F32R), sb("wqk_lo", [P, DC, D], F32R)
        woT = sb("woT", [P, DC, D])
        wT = sb("wT", [P, DC, D], F32R)
        vec_rows = sb("vec_rows", [4 * DC, P])
        vec_cols = sb("vec_cols", [P, 4 * DC])
        bk_wide = sb("bk_wide", [P, DC, P])
        derived = sb("derived", [P, DC + 1])
        u_wide = sb("u_wide", [P, D])
        bo_sb, bo_g = sb("bo_sb", [P, 1, D]), sb("bo_g", [P, 1, D])
        gates, tanh_g = sb("gates", [P, 2]), sb("tanh_g", [P, 2])
        ident, minus_half = sb("ident", [P, P]), sb("minus_half", [P, GB])
        bqT, bkT, scT, biT = (vec_cols[:, k * DC:(k + 1) * DC] for k in range(4))
        ybias, bqbk = derived[:, 0:DC], derived[:, DC:DC + 1]
        ps_vec = o_bank[:, 0:4 * DC]
        ps_derived, ps_u = o_bank[:, 16:17 + DC], o_bank[:, D:2 * D]

        x_loaded, ctx_loaded = [sem(f"x_loaded{g}") for g in range(G)], [sem(f"ctx_loaded{g}") for g in range(G)]
        wqk_loaded, vecs_loaded, wo_loaded, w_loaded = (sem(n) for n in ("wqk_loaded", "vecs_loaded", "wo_loaded", "w_loaded"))
        gates_loaded, bo_loaded, mask_loaded, stored = (sem(n) for n in ("gates_loaded", "bo_loaded", "mask_loaded", "stored"))
        zeroed, ident_ready, half_ready, mask_ready, tanh_ready = (
            sem(n) for n in ("zeroed", "ident_ready", "half_ready", "mask_ready", "tanh_ready"))
        bo_g_ready, sign2_ready, ps_vec_ready, vec_ready, bk_wide_ready = (
            sem(n) for n in ("bo_g_ready", "sign2_ready", "ps_vec_ready", "vec_ready", "bk_wide_ready"))
        ps_wqk_ready, wqk_ready, ps_derived_ready, derived_ready = (
            sem(n) for n in ("ps_wqk_ready", "wqk_ready", "ps_derived_ready", "derived_ready"))
        ps_woT_ready, woT_ready, wqk_lo_ready, u_ready, ps_wT_ready, wT_ready = (
            sem(n) for n in ("ps_woT_ready", "woT_ready", "wqk_lo_ready", "u_ready", "ps_wT_ready", "wT_ready"))
        xT_prod, cT_prod, Z_prod, PT_prod, x1T_prod, outT_prod = (
            sem(n) for n in ("xT_prod", "cT_prod", "Z_prod", "PT_prod", "x1T_prod", "outT_prod"))
        Y_prod, S_prod, O_prod, F_prod = (sem(n) for n in ("Y_prod", "S_prod", "O_prod", "F_prod")) 
        bn_x_done, mv_x_done, ve_x_done, rstd_x_done, mr_x_done, nmr_x_done, xn_done = (
            sem(n) for n in ("bn_x_done", "mv_x_done", "ve_x_done", "rstd_x_done", "mr_x_done", "nmr_x_done", "xn_done"))
        bn_1_done, mv_1_done, ve_1_done, rstd_1_done, x1n_done = (
            sem(n) for n in ("bn_1_done", "mv_1_done", "ve_1_done", "rstd_1_done", "x1n_done"))
        xb_done, xT_hi_done, xT_lo_done, cT_done, r_done = (
            sem(n) for n in ("xb_done", "xT_hi_done", "xT_lo_done", "cT_done", "r_done"))
        Y_done, Z_done, t_done, smax_r_done, shift_done = (
            sem(n) for n in ("Y_done", "Z_done", "t_done", "smax_r_done", "shift_done"))
        p_done, PT_done, recip_done, x1_done = (sem(n) for n in ("p_done", "PT_done", "recip_done", "x1_done"))
        x1T_hi_done, x1T_lo_done, f_done, f_clip_done, out_done = (
            sem(n) for n in ("x1T_hi_done", "x1T_lo_done", "f_done", "f_clip_done", "out_done"))

        rows = lambda g: slice(g * GB, (g + 1) * GB)
        block = stack.enter_context(nc.Block())

        @block.sync
        def _(sp):
            def load_x(g):
                sp.dma_start(x_sb[:, rows(g), :], x_rows[:, rows(g), :]).then_inc(x_loaded[g], 16)

            def load_ctx(g):
                sp.dma_start(ctx_sb[:, rows(g), :], ctx_rows[:, rows(g), :]).then_inc(ctx_loaded[g], 16)

            load_x(0)
            sp.dma_start(wq_sb[:], wq.rearrange("(c p) d -> p c d", p=P)).then_inc(wqk_loaded, 16)
            sp.dma_start(wk_sb[:], wk.rearrange("(c p) d -> p c d", p=P)).then_inc(wqk_loaded, 16)
            load_ctx(0)
            load_x(1)
            sp.dma_start(wo_sb[:], wo.rearrange("(c p) d -> p c d", p=P)).then_inc(wo_loaded, 16)
            for k, v in enumerate((g_xattn, g_ffn)):
                sp.dma_start(gates[:, k:k + 1], v.rearrange("(o d) -> o d", o=1).to_broadcast([P, 1])
                              ).then_inc(gates_loaded, 16)
            sp.dma_start(mask_u8[:], mask.rearrange("(o b) k -> o b k", o=1).to_broadcast([P, B, P])
                          ).then_inc(mask_loaded, 16)
            sp.dma_start(bo_sb[:, 0, :], bo.rearrange("(o d) -> o d", o=1).to_broadcast([P, D])).then_inc(bo_loaded, 16)
            load_ctx(1)
            sp.dma_start(w_sb[:], w_ffn.rearrange("(c p) d -> p c d", p=P)).then_inc(w_loaded, 16)
            for g in range(2, G):
                load_x(g)
                load_ctx(g)
            for g in range(G):
                sp.wait_ge(out_done, g + 1)
                sp.dma_start(out_rows[:, rows(g), :], out_sb[:, rows(g), :]).then_inc(stored, 16)
            sp.wait_ge(stored, 16 * G)

        @block.scalar
        def _(act):
            for k, v in enumerate((bq, bk, scale_ffn, bias_ffn)):
                act.dma_start(vec_rows[k * DC:(k + 1) * DC, :], v.rearrange("(c p) -> c p", p=P)).then_inc(vecs_loaded, 16)

            def evict_xT_hi(g):
                act.wait_ge(xT_prod, g + 1)
                nc.scalar.copy(xT_hi[:, g % 2], ps_xT).then_inc(xT_hi_done, 1)

            def evict_cT(g):
                act.wait_ge(cT_prod, g + 1)
                nc.scalar.copy(cT[:, g % 2], ps_cT).then_inc(cT_done, 1)

            def evict_x1T_hi(g):
                act.wait_ge(x1T_prod, g + 1)
                nc.scalar.copy(x1T_hi[:, g % 2], ps_x1T).then_inc(x1T_hi_done, 1)

            def evict_Y(g):
                act.wait_ge(Y_prod, g + 1)
                if g == 0:
                    act.wait_ge(derived_ready, 1)
                for c in range(DC):
                    nc.scalar.activation(Y_sb[:, g % 2, c], ps_Y[:, c], ACT.Identity, bias=ybias[:, c:c + 1]
                                         ).then_inc(Y_done, 1)

            def evict_PT(g):
                act.wait_ge(PT_prod, g + 1)
                nc.scalar.copy(PT_sb[:, g % 2], ps_PT).then_inc(PT_done, 1)

            def evict_Z(g):
                act.wait_ge(Z_prod, g + 1)
                nc.scalar.copy(Z_sb[:, g % 2], ps_Z).then_inc(Z_done, 1)

            def exp(g):
                act.wait_ge(shift_done, g + 1)
                for b in range(GB):
                    nc.scalar.activation(p_sb[:, g % 2, b], t_sb[:, g % 2, b], ACT.Exp,
                                         bias=shift[:, g * GB + b:g * GB + b + 1],
                                         accum_out=psum_p[:, g * GB + b:g * GB + b + 1]).then_inc(p_done, 1)

            def ffn_affine(g):
                act.wait_ge(F_prod, g + 1)
                for c in range(DC):
                    nc.scalar.activation(f_sb[:, g % 2, c], ps_F[:, c], ACT.Identity, bias=biT[:, c:c + 1],
                                         scale=scT[:, c:c + 1]).then_inc(f_done, 1)

            act.wait_ge(ps_wqk_ready, 1)
            nc.scalar.copy(wqk_hi[:], ps_Y).then_inc(wqk_ready, 1)
            evict_xT_hi(0)
            evict_cT(0)
            act.wait_ge(gates_loaded, 32)
            nc.scalar.activation(tanh_g[:], gates[:], ACT.Tanh).then_inc(tanh_ready, 1)
            evict_Y(0)
            act.wait_ge(ps_woT_ready, 1)
            act.wait_ge(tanh_ready, 1)
            nc.scalar.activation(woT[:], ps_Z, ACT.Identity, scale=tanh_g[:, 0:1]).then_inc(woT_ready, 1)
            for i in range(G + 2):
                if 1 <= i <= G:
                    evict_PT(i - 1)
                if i >= 2:
                    evict_x1T_hi(i - 2)
                if i + 1 < G:
                    evict_cT(i + 1)
                if 1 <= i < G:
                    evict_Y(i)
                if i >= 2:
                    ffn_affine(i - 2)
                if i < G:
                    exp(i)
                    evict_Z(i)
                if i + 1 < G:
                    evict_xT_hi(i + 1)

        @block.gpsimd
        def _(pool):
            nc.gpsimd.memset(ident[:], 0.0).then_inc(zeroed, 1)
            nc.gpsimd.memset(minus_half[:], -0.5).then_inc(half_ready, 1)
            pool.wait_ge(zeroed, 1)
            nc.gpsimd.affine_select(out=ident[:], in_=ident[:], compare_op=ALU.not_equal, fill=1.0, base=0,
                                    pattern=[[-1, P]], channel_multiplier=1).then_inc(ident_ready, 1)

            def rstd_1s(g):
                pool.wait_ge(ve_1_done, g + 1)
                nc.gpsimd.tensor_tensor(rstd_1[:, rows(g)], ve_1[:, rows(g)], minus_half[:], ALU.pow).then_inc(rstd_1_done, 1)

            def norm_x(g):
                pool.wait_ge(ve_x_done, g + 1)
                nc.gpsimd.tensor_tensor(rstd_x[:, rows(g)], ve_x[:, rows(g)], minus_half[:], ALU.pow).then_inc(rstd_x_done, 1)
                pool.wait_ge(rstd_x_done, g + 1)
                nc.gpsimd.tensor_tensor(mr_x[:, rows(g)], mv_x[:, rows(g), 0], rstd_x[:, rows(g)], ALU.mult).then_inc(mr_x_done, 1)
                pool.wait_ge(mr_x_done, g + 1)
                nc.gpsimd.tensor_scalar(nmr_x[:, rows(g)], mr_x[:, rows(g)], -1.0, None, ALU.mult).then_inc(nmr_x_done, 1)
                pool.wait_ge(nmr_x_done, g + 1)
                if g >= 3:
                    pool.wait_ge(xT_prod, g - 2)
                    pool.wait_ge(r_done, GB * (g - 2))
                for b in range(GB):
                    r = g * GB + b
                    nc.gpsimd.tensor_scalar(xn[:, g % 3, b], x_sb[:, r], rstd_x[:, r:r + 1], nmr_x[:, r:r + 1],
                                            ALU.mult, ALU.add).then_inc(xn_done, 1)

            def mask_terms(g):
                nc.gpsimd.tensor_scalar(mask_add[:, rows(g)], mask_u8[:, rows(g)], MASKED, 1.0, ALU.mult, ALU.mult
                                        ).then_inc(mask_ready, 1)

            def add_bo(g):
                for b in range(GB):
                    r = g * GB + b
                    nc.gpsimd.tensor_tensor(xb_sb[:, r], x_sb[:, r], bo_g[:, 0], ALU.add).then_inc(xb_done, 1)

            pool.wait_ge(half_ready, 1)
            norm_x(0)
            pool.wait_ge(mask_loaded, 16)
            mask_terms(0)
            norm_x(1)
            pool.wait_ge(tanh_ready, 1)
            pool.wait_ge(bo_loaded, 16)
            nc.gpsimd.tensor_scalar(bo_g[:], bo_sb[:], tanh_g[:, 0:1], 1.0, ALU.mult, ALU.mult).then_inc(bo_g_ready, 1)
            pool.wait_ge(bo_g_ready, 1)
            for i in range(G + 1):
                if i >= 1:
                    rstd_1s(i - 1)
                if i < G:
                    add_bo(i)
                if i + 1 < G:
                    mask_terms(i + 1)
                if i + 2 < G:
                    norm_x(i + 2)

        @block.vector
        def _(dve):
            def stats_x(g):
                dve.wait_ge(x_loaded[g], 16)
                for b in range(GB):
                    nc.vector.bn_stats(bn_x[:, g * GB + b], x_sb[:, g * GB + b]).then_inc(bn_x_done, 1)
                for b in range(GB):
                    dve.wait_ge(bn_x_done, GB * g + b + 1)
                    nc.vector.bn_aggr(mv_x[:, g * GB + b], bn_x[:, g * GB + b]).then_inc(mv_x_done, 1)
                dve.wait_ge(mv_x_done, GB * (g + 1))
                nc.vector.tensor_scalar(ve_x[:, rows(g)], mv_x[:, rows(g), 1], EPS, None, ALU.add).then_inc(ve_x_done, 1)

            def stats_x1(g):
                for b in range(GB):
                    dve.wait_ge(x1_done, GB * g + b + 1)
                    nc.vector.bn_stats(bn_1[:, g * GB + b], x1_sb[:, g * GB + b]).then_inc(bn_1_done, 1)
                for b in range(GB):
                    dve.wait_ge(bn_1_done, GB * g + b + 1)
                    nc.vector.bn_aggr(mv_1[:, g * GB + b], bn_1[:, g * GB + b]).then_inc(mv_1_done, 1)
                dve.wait_ge(mv_1_done, GB * (g + 1))
                nc.vector.tensor_scalar(ve_1[:, rows(g)], mv_1[:, rows(g), 1], EPS, None, ALU.add).then_inc(ve_1_done, 1)

            def split_xT(g):
                dve.wait_ge(xT_hi_done, g + 1)
                nc.vector.tensor_tensor(xT_lo[:, g % 2], ps_xT, xT_hi[:, g % 2].bitcast(F32), ALU.subtract
                                        ).then_inc(xT_lo_done, 1)

            def split_x1T(g):
                dve.wait_ge(x1T_hi_done, g + 1)
                nc.vector.tensor_tensor(x1T_lo[:, g % 2], ps_x1T, x1T_hi[:, g % 2].bitcast(F32), ALU.subtract
                                        ).then_inc(x1T_lo_done, 1)

            def norm_x1(g):
                dve.wait_ge(rstd_1_done, g + 1)
                for b in range(GB):
                    r = g * GB + b
                    nc.vector.tensor_scalar(x1n[:, g % 2, b], x1_sb[:, r], mv_1[:, r, 0:1], rstd_1[:, r:r + 1],
                                            ALU.subtract, ALU.mult).then_inc(x1n_done, 1)

            def dot_u(g):
                dve.wait_ge(xn_done, GB * (g + 1))
                for b in range(GB):
                    r = g * GB + b
                    nc.vector.tensor_tensor_reduce(x_dot_u[:, g % 2, b], xn[:, g % 3, b], u_wide[:], 1.0, bqbk,
                                                   ALU.mult, ALU.add, r_sb[:, r:r + 1]).then_inc(r_done, 1)

            def clip(g):
                dve.wait_ge(f_done, DC * (g + 1))
                nc.vector.tensor_scalar(f_clip[:, g % 2], f_sb[:, g % 2], CLIP, -CLIP, ALU.min, ALU.max
                                        ).then_inc(f_clip_done, 1)

            def mask_and_max(g):
                dve.wait_ge(mask_ready, g + 1)
                dve.wait_ge(S_prod, g + 1)
                for b in range(GB):
                    r = g * GB + b
                    nc.vector.tensor_tensor_reduce(t_sb[:, g % 2, b], ps_S[:, b], mask_add[:, r], 1.0, FLOOR,
                                                   ALU.add, ALU.max, smax[:, r:r + 1]).then_inc(t_done, 1)
                dve.wait_ge(t_done, GB * (g + 1))
                dve.wait_ge(r_done, GB * (g + 1))
                nc.vector.tensor_tensor(smax_r[:, rows(g)], smax[:, rows(g)], r_sb[:, rows(g)], ALU.add
                                        ).then_inc(smax_r_done, 1)
                dve.wait_ge(smax_r_done, g + 1)
                nc.vector.tensor_tensor(shift[:, rows(g)], r_sb[:, rows(g)], smax_r[:, rows(g)], ALU.subtract
                                        ).then_inc(shift_done, 1)

            def residual(g):
                dve.wait_ge(p_done, GB * (g + 1))
                nc.vector.reciprocal(recip_p[:, rows(g)], psum_p[:, rows(g)]).then_inc(recip_done, 1)
                dve.wait_ge(recip_done, g + 1)
                dve.wait_ge(xb_done, GB * (g + 1))
                dve.wait_ge(O_prod, g + 1)
                for b in range(GB):
                    r = g * GB + b
                    nc.vector.scalar_tensor_tensor(out=x1_sb[:, r], in0=ps_O[:, b], scalar=recip_p[:, r:r + 1],
                                                   in1=xb_sb[:, r], op0=ALU.mult, op1=ALU.add).then_inc(x1_done, 1)

            def final(g):
                dve.wait_ge(outT_prod, g + 1)
                nc.vector.scalar_tensor_tensor(out=out_sb[:, rows(g)], in0=ps_Fr, scalar=tanh_g[:, 1:2],
                                               in1=x1_sb[:, rows(g)], op0=ALU.mult, op1=ALU.add).then_inc(out_done, 1)

            stats_x(0)
            dve.wait_ge(ps_vec_ready, 1)
            nc.vector.tensor_copy(vec_cols[:], ps_vec).then_inc(vec_ready, 1)
            dve.wait_ge(vec_ready, 1)
            for c in range(DC):
                nc.vector.tensor_copy(bk_wide[:, c], bkT[:, c:c + 1].to_broadcast([P, P])).then_inc(bk_wide_ready, 1)
            dve.wait_ge(wqk_ready, 1)
            nc.vector.tensor_tensor(wqk_lo[:], ps_Y, wqk_hi[:].bitcast(F32), ALU.subtract).then_inc(wqk_lo_ready, 1)
            split_xT(0)
            stats_x(1)
            dve.wait_ge(ps_derived_ready, 1)
            nc.vector.tensor_copy(derived[:], ps_derived).then_inc(derived_ready, 1)
            nc.vector.tensor_copy(u_wide[:], ps_u).then_inc(u_ready, 1)
            dve.wait_ge(u_ready, 1)
            for i in range(G + 2):
                if 3 <= i <= G:
                    final(i - 3)
                if i >= 2:
                    split_x1T(i - 2)
                if 1 <= i <= G:
                    residual(i - 1)
                    stats_x1(i - 1)
                if i < G:
                    dot_u(i)
                if i >= G:
                    clip(i - 2)
                if i < G:
                    mask_and_max(i)
                if 1 <= i <= G:
                    norm_x1(i - 1)
                if 2 <= i < G:
                    clip(i - 2)
                if i + 2 < G:
                    stats_x(i + 2)
                if i == 0:
                    dve.wait_ge(w_loaded, 16)
                    nc.vector.tensor_scalar(w_sign2[:], w_sb[:], 0.0, 2.0, ALU.is_ge, ALU.mult).then_inc(sign2_ready, 1)
                if i == 1:
                    dve.wait_ge(ps_wT_ready, 1)
                    nc.vector.tensor_scalar(wT[:], ps_F, 1.0, None, ALU.subtract).then_inc(wT_ready, 1)
                if i >= G:
                    final(i - 2)
                if i + 1 < G:
                    split_xT(i + 1)

        @block.tensor
        def _(pe):
            def transposes(dst, src):
                for b in range(GB):
                    for c in range(DC):
                        last = nc.tensor.transpose(dst[:, c, b * P:(b + 1) * P], src[:, b, c * P:(c + 1) * P], ident[:])
                return last

            def split_matmuls(dst, pairs):
                for n, (lhsT, rhs) in enumerate(pairs):
                    last = nc.tensor.matmul(dst, lhsT, rhs, start=(n == 0), stop=(n == len(pairs) - 1))
                return last

            def transpose_x(g):
                pe.wait_ge(xn_done, GB * (g + 1))
                if g >= 1:
                    pe.wait_ge(xT_lo_done, g)
                transposes(ps_xT, xn[:, g % 3]).then_inc(xT_prod, 1)

            def transpose_ctx(g):
                pe.wait_ge(ctx_loaded[g], 16)
                if g >= 1:
                    pe.wait_ge(cT_done, g)
                transposes(ps_cT, ctx_sb[:, rows(g)]).then_inc(cT_prod, 1)

            def transpose_x1(g):
                pe.wait_ge(x1n_done, GB * (g + 1))
                if g >= 1:
                    pe.wait_ge(x1T_lo_done, g)
                transposes(ps_x1T, x1n[:, g % 2]).then_inc(x1T_prod, 1)

            def project_Y(g):
                pe.wait_ge(xT_lo_done, g + 1)
                if g >= 1:
                    pe.wait_ge(Y_done, DC * g)
                else:
                    pe.wait_ge(wqk_lo_ready, 1)
                for m in range(DC):
                    pairs = []
                    for c in range(DC):
                        w_hi, w_lo = (w[:, c, m * P:(m + 1) * P] for w in (wqk_hi, wqk_lo))
                        pairs += [(w_hi, xT_hi[:, g % 2, c]), (w_hi, xT_lo[:, g % 2, c]), (w_lo, xT_hi[:, g % 2, c])]
                    last = split_matmuls(ps_Y[:, m], pairs)
                last.then_inc(Y_prod, 1)

            def project_Z(g):
                pe.wait_ge(cT_done, g + 1)
                if g >= 1:
                    pe.wait_ge(Z_done, g)
                else:
                    pe.wait_ge(woT_ready, 1)
                for b in range(GB):
                    last = split_matmuls(ps_Z[:, b], [(cT[:, g % 2, c, b * P:(b + 1) * P], woT[:, c]) for c in range(DC)])
                last.then_inc(Z_prod, 1)

            def scores(g):
                pe.wait_ge(cT_done, g + 1)
                if g >= 1:
                    pe.wait_ge(PT_done, g)
                for b in range(GB):
                    for c in range(DC):
                        if b == 0:
                            pe.wait_ge(Y_done, DC * g + c + 1)
                        last = nc.tensor.matmul(ps_S[:, b], Y_sb[:, g % 2, c, b * P:(b + 1) * P],
                                                cT[:, g % 2, c, b * P:(b + 1) * P], start=(c == 0), stop=(c == DC - 1))
                last.then_inc(S_prod, 1)

            def transpose_p(g):
                pe.wait_ge(p_done, GB * (g + 1))
                if g >= 1:
                    pe.wait_ge(PT_done, g)
                for b in range(GB):
                    last = nc.tensor.transpose(ps_PT[:, b], p_sb[:, g % 2, b], ident[:])
                last.then_inc(PT_prod, 1)

            def attend(g):
                pe.wait_ge(PT_done, g + 1)
                pe.wait_ge(Z_done, g + 1)
                if g >= 1:
                    pe.wait_ge(x1_done, GB * g)
                for b in range(GB):
                    last = nc.tensor.matmul(ps_O[:, b], PT_sb[:, g % 2, b], Z_sb[:, g % 2, b], start=True, stop=True)
                last.then_inc(O_prod, 1)

            def ffn(g):
                pe.wait_ge(x1T_lo_done, g + 1)
                if g >= 1:
                    pe.wait_ge(out_done, g)
                else:
                    pe.wait_ge(wT_ready, 1)
                for m in range(DC):
                    pairs = []
                    for c in range(DC):
                        pairs += [(wT[:, c, m * P:(m + 1) * P], t[:, g % 2, c]) for t in (x1T_hi, x1T_lo)]
                    last = split_matmuls(ps_F[:, m], pairs)
                last.then_inc(F_prod, 1)

            def transpose_out(g):
                pe.wait_ge(f_clip_done, g + 1)
                for b in range(GB):
                    for c in range(DC):
                        last = nc.tensor.transpose(ps_Fr[:, b, c * P:(c + 1) * P], f_clip[:, g % 2, c, b * P:(b + 1) * P],
                                                   ident[:])
                last.then_inc(outT_prod, 1)

            pe.wait_ge(ident_ready, 1)
            for _ in range(WARM_UP):
                nc.tensor.transpose(ps_F[:, 0, 0:P], ident[:], ident[:])
            pe.wait_ge(wqk_loaded, 32)
            for m in range(DC):
                last = split_matmuls(ps_Y[:, m], [(wq_sb[:, e, m * P:(m + 1) * P], wk_sb[:, e]) for e in range(DC)])
                if m == 0:
                    pe.wait_ge(vecs_loaded, 16 * 4)
                    nc.tensor.transpose(ps_vec, vec_rows[:], ident[0:4 * DC, 0:4 * DC]).then_inc(ps_vec_ready, 1)
            last.then_inc(ps_wqk_ready, 1)
            transpose_x(0)
            transpose_ctx(0)
            pe.wait_ge(bk_wide_ready, DC)
            for m in range(DC):
                split_matmuls(ps_derived[:, m:m + 1], [(wk_sb[:, e, m * P:(m + 1) * P], bqT[:, e:e + 1]) for e in range(DC)])
            split_matmuls(ps_derived[:, DC:DC + 1], [(bk_wide[:, e], bqT[:, e:e + 1]) for e in range(DC)])
            split_matmuls(ps_u, [(bk_wide[:, e], wq_sb[:, e]) for e in range(DC)]).then_inc(ps_derived_ready, 1)
            project_Y(0)
            pe.wait_ge(wo_loaded, 16)
            transposes(ps_Z, wo_sb).then_inc(ps_woT_ready, 1)
            for i in range(G + 2):
                if 1 <= i <= G:
                    transpose_p(i - 1)
                if 3 <= i <= G:
                    transpose_out(i - 3)
                if i + 1 < G:
                    transpose_ctx(i + 1)
                if 1 <= i <= G:
                    attend(i - 1)
                if 1 <= i < G:
                    project_Y(i)
                if i == 1:
                    pe.wait_ge(sign2_ready, 1)
                    transposes(ps_F, w_sign2).then_inc(ps_wT_ready, 1)
                if i >= 2:
                    ffn(i - 2)
                if i < G:
                    scores(i)
                    project_Z(i)
                if i >= G:
                    transpose_out(i - 2)
                if i + 1 < G:
                    transpose_x(i + 1)
                if 1 <= i <= G:
                    transpose_x1(i - 1)


_INS = ['x', 'ctx_1024', 'mask_BxS2_bk0', 'g_xattn', 'g_ffn', 'L0_xattn_Wq', 'L0_xattn_bq', 'L0_xattn_Wk', 'L0_xattn_bk',
        'L0_xattn_Wo', 'L0_xattn_bo', 'L0_ffn_weights', 'L0_ffn_scale', 'L0_ffn_bias']
_OUTS = [((16, 128, 256), 'float32')]


def kernel(**inputs):
    import numpy as _np
    import concourse.bacc as _bacc
    from concourse import mybir as _mybir
    from concourse.bass_utils import run_bass_kernel_spmd as _run

    nc = _bacc.Bacc("TRN2", target_bir_lowering=False, num_devices=1)
    arrays, args = {}, []
    for name in _INS:
        a = _np.ascontiguousarray(inputs[name])
        arrays[f"in_{name}_dram"] = a
        args.append(nc.dram_tensor(f"in_{name}_dram", a.shape, _mybir.dt.from_np(a.dtype), kind="ExternalInput").ap())
    for i, (shape, dtype) in enumerate(_OUTS):
        dt = _mybir.dt.from_np(_np.dtype(dtype))
        args.append(nc.dram_tensor(f"out_{i}_dram", shape, dt, kind="ExternalOutput").ap())
    gated_xattn_ffn(nc, *args)
    r = _run(nc, [arrays], core_ids=[0])
    got = tuple(r.results[0][f"out_{i}_dram"] for i in range(len(_OUTS)))
    return got[0]
```
